# Optimizing a Trainium2 kernel written in Bass

```python
import numpy as np
import jax
import jax.numpy as jnp

def _softmax(x, axis=-1):
    return jax.nn.softmax(x, axis=axis)

def _gelu(x):
    return jax.nn.gelu(x, approximate=True)

def _silu(x):
    return jax.nn.silu(x)

def _sigmoid(x):
    return jax.nn.sigmoid(x)

def _layernorm(x, axis=-1, eps=1e-05):
    m = jnp.mean(x, axis=axis, keepdims=True)
    v = jnp.var(x, axis=axis, keepdims=True)
    return (x - m) / jnp.sqrt(v + eps)

def _scatter_add(tgt, idx, src, axis=0):
    return tgt.at[idx].add(src)

def _segment_sum(src, seg, n):
    return jax.ops.segment_sum(src, seg, n)
kernel_name = 'mk_macaron_d1_jaxref_r8_af24dc'

def setup_inputs(seed: int=0):
    np.random.seed(seed)
    _w = jnp.asarray

    def _L0_attn_setup():
        import jax, jax.numpy as jnp
        import numpy as np
        B, T, D, H = (4, 256, 128, 16)
        HD = D // H

        def l2_norm(x, eps=1e-12):
            return x / jnp.maximum(jnp.linalg.norm(x, axis=-1, keepdims=True), eps)
        key = jax.random.key(seed)
        ks = jax.random.split(key, 11)
        std = 0.02
        w = lambda k, shape: jax.random.normal(k, shape, jnp.float32) * std
        return dict(x=jax.random.normal(ks[0], (B, T, D), jnp.float32), Wq=w(ks[1], (D, D)), Wk=w(ks[2], (D, D)), Wv=w(ks[3], (D, D)), Wgamma=w(ks[4], (D, H)), Wf1=w(ks[5], (D, HD)), Wf2=w(ks[6], (HD, D)), Wog1=w(ks[7], (D, HD)), Wog2=w(ks[8], (HD, D)), norm_w=jnp.ones((D,), jnp.float32), Wo=w(ks[9], (D, D)))
    _L0_attn_in = _L0_attn_setup()

    def _L0_ffn_setup():
        import jax, jax.numpy as jnp
        import numpy as np
        D_MODEL = 128
        HIDDEN = 512
        N_ROUTING = 2
        key = jax.random.key(seed)
        ks = jax.random.split(key, 10)
        s = 0.02
        x = jax.random.normal(ks[0], (4, 512, D_MODEL), dtype=jnp.float32)
        gate_w = jax.random.normal(ks[1], (N_ROUTING, D_MODEL), dtype=jnp.float32) * s
        w1 = jax.random.normal(ks[2], (N_ROUTING, D_MODEL, HIDDEN), dtype=jnp.float32) * s
        b1 = jax.random.normal(ks[3], (N_ROUTING, HIDDEN), dtype=jnp.float32) * s
        w2 = jax.random.normal(ks[4], (N_ROUTING, HIDDEN, D_MODEL), dtype=jnp.float32) * s
        b2 = jax.random.normal(ks[5], (N_ROUTING, D_MODEL), dtype=jnp.float32) * s
        sw1 = jax.random.normal(ks[6], (D_MODEL, HIDDEN), dtype=jnp.float32) * s
        sb1 = jax.random.normal(ks[7], (HIDDEN,), dtype=jnp.float32) * s
        sw2 = jax.random.normal(ks[8], (HIDDEN, D_MODEL), dtype=jnp.float32) * s
        sb2 = jax.random.normal(ks[9], (D_MODEL,), dtype=jnp.float32) * s
        return {'x': x, 'gate_w': gate_w, 'w1': w1, 'b1': b1, 'w2': w2, 'b2': b2, 'sw1': sw1, 'sb1': sb1, 'sw2': sw2, 'sb2': sb2}
    _L0_ffn_in = _L0_ffn_setup()
    _d = {'L0_attn_x': _L0_attn_in['x'], 'L0_attn_Wq': _L0_attn_in['Wq'], 'L0_attn_Wk': _L0_attn_in['Wk'], 'L0_attn_Wv': _L0_attn_in['Wv'], 'L0_attn_Wgamma': _L0_attn_in['Wgamma'], 'L0_attn_Wf1': _L0_attn_in['Wf1'], 'L0_attn_Wf2': _L0_attn_in['Wf2'], 'L0_attn_Wog1': _L0_attn_in['Wog1'], 'L0_attn_Wog2': _L0_attn_in['Wog2'], 'L0_attn_norm_w': _L0_attn_in['norm_w'], 'L0_attn_Wo': _L0_attn_in['Wo'], 'L0_ffn_gate_w': _L0_ffn_in['gate_w'], 'L0_ffn_w1': _L0_ffn_in['w1'], 'L0_ffn_b1': _L0_ffn_in['b1'], 'L0_ffn_w2': _L0_ffn_in['w2'], 'L0_ffn_b2': _L0_ffn_in['b2'], 'L0_ffn_sw1': _L0_ffn_in['sw1'], 'L0_ffn_sb1': _L0_ffn_in['sb1'], 'L0_ffn_sw2': _L0_ffn_in['sw2'], 'L0_ffn_sb2': _L0_ffn_in['sb2']}
    _x0 = _d['L0_attn_x']
    _d['L0_attn_x'] = jax.random.normal(jax.random.fold_in(jax.random.key(seed), 1), (4, 512, 128), dtype=_x0.dtype)
    del _x0
    return _d

def reference(L0_attn_x, L0_attn_Wq, L0_attn_Wk, L0_attn_Wv, L0_attn_Wgamma, L0_attn_Wf1, L0_attn_Wf2, L0_attn_Wog1, L0_attn_Wog2, L0_attn_norm_w, L0_attn_Wo, L0_ffn_gate_w, L0_ffn_w1, L0_ffn_b1, L0_ffn_w2, L0_ffn_b2, L0_ffn_sw1, L0_ffn_sb1, L0_ffn_sw2, L0_ffn_sb2):

    def _L0_attn_ref(x, Wq, Wk, Wv, Wgamma, Wf1, Wf2, Wog1, Wog2, norm_w, Wo):
        import jax, jax.numpy as jnp
        import numpy as np
        B, T, D, H = (4, 256, 128, 16)
        HD = D // H

        def l2_norm(x, eps=1e-12):
            return x / jnp.maximum(jnp.linalg.norm(x, axis=-1, keepdims=True), eps)
        b, n, d = x.shape
        q = jax.nn.silu(x @ Wq)
        k = jax.nn.silu(x @ Wk)
        v = x @ Wv
        log_f = jax.nn.log_sigmoid(x @ Wf1 @ Wf2)
        gamma = -jax.nn.sigmoid(x @ Wgamma)
        q = q.reshape(b, n, H, HD)
        k = l2_norm(k.reshape(b, n, H, HD))
        v = v.reshape(b, n, H, HD)
        gk = log_f.reshape(b, n, H, HD)
        a = k * gamma[..., None] * jnp.exp(gk)

        def step(S, inp):
            qt, kt, vt, at, gkt = inp
            S = S * jnp.exp(gkt)[..., None]
            sab = jnp.einsum('bhk,bhkv->bhv', at, S)
            S = S + kt[..., None] * (sab[..., None, :] + vt[..., None, :])
            ot = jnp.einsum('bhk,bhkv->bhv', qt, S)
            return (S, ot)
        seq = tuple((jnp.moveaxis(t, 1, 0) for t in (q, k, v, a, gk)))
        S0 = jnp.zeros((b, H, HD, HD), x.dtype)
        _, o = jax.lax.scan(step, S0, seq)
        o = jnp.moveaxis(o, 0, 1).reshape(b, n, d)
        o = o * jax.nn.sigmoid(x @ Wog1 @ Wog2)
        mu = o.mean(-1, keepdims=True)
        var = ((o - mu) ** 2).mean(-1, keepdims=True)
        o = (o - mu) * jax.lax.rsqrt(var + 1e-05) * norm_w
        return o @ Wo

    def _L0_ffn_ref(x, gate_w, w1, b1, w2, b2, sw1, sb1, sw2, sb2):
        import jax, jax.numpy as jnp
        import numpy as np
        D_MODEL = 128
        HIDDEN = 512
        N_ROUTING = 2
        B, S, D = x.shape
        xf = x.reshape(-1, D)
        gate_scores = xf @ gate_w.T
        gate_probs = jax.nn.softmax(gate_scores, axis=-1)
        top1 = jnp.argmax(gate_probs, axis=-1)
        one_hot = jax.nn.one_hot(top1, N_ROUTING, dtype=xf.dtype)
        masked = xf[None, :, :] * one_hot.T[:, :, None]
        h = jax.nn.relu(jnp.einsum('end,edh->enh', masked, w1) + b1[:, None, :])
        expert_out = jnp.einsum('enh,ehd->end', h, w2) + b2[:, None, :]
        routing_output = expert_out.sum(axis=0)
        shared = jax.nn.relu(xf @ sw1 + sb1) @ sw2 + sb2
        return (routing_output + shared).reshape(B, S, D)
    x = L0_attn_x
    x = x + 0.5 * _L0_ffn_ref(_layernorm(x, axis=-1), L0_ffn_gate_w, L0_ffn_w1, L0_ffn_b1, L0_ffn_w2, L0_ffn_b2, L0_ffn_sw1, L0_ffn_sb1, L0_ffn_sw2, L0_ffn_sb2)
    x = x + _L0_attn_ref(_layernorm(x, axis=-1), L0_attn_Wq, L0_attn_Wk, L0_attn_Wv, L0_attn_Wgamma, L0_attn_Wf1, L0_attn_Wf2, L0_attn_Wog1, L0_attn_Wog2, L0_attn_norm_w, L0_attn_Wo)
    x = x + 0.5 * _L0_ffn_ref(_layernorm(x, axis=-1), L0_ffn_gate_w, L0_ffn_w1, L0_ffn_b1, L0_ffn_w2, L0_ffn_b2, L0_ffn_sw1, L0_ffn_sb1, L0_ffn_sw2, L0_ffn_sb2)
    return x

_drawn_inputs = setup_inputs


def setup_inputs(seed=0):
    import zlib

    import numpy as np

    out = dict(_drawn_inputs(seed))
    spreads = {'L0_attn_norm_w': (1.0, 0.2)}
    factors = {'L0_attn_Wgamma': 8.0,
     'L0_attn_Wf1': 8.0,
     'L0_attn_Wf2': 8.0,
     'L0_attn_Wog1': 8.0,
     'L0_attn_Wog2': 8.0,
     'L0_ffn_b1': 7.306,
     'L0_ffn_sb1': 8.0}
    for name, (base, spread) in spreads.items():
        noise = np.random.default_rng([zlib.crc32(name.encode()), seed]).standard_normal(out[name].shape)
        drawn = base * np.exp(spread * noise) if base else spread * noise
        out[name] = jnp.asarray(drawn.astype(out[name].dtype))
    for name, factor in factors.items():
        out[name] = (out[name] * factor).astype(out[name].dtype)
    return out
```

```python
from contextlib import ExitStack

import concourse.bass as bass
from concourse import mybir

F32 = mybir.dt.float32
ALU = mybir.AluOpType
ACT = mybir.ActivationFunctionType
AX = mybir.AxisListType

P = 128
B, T, D = 4, 512, 128
H, HD = 16, 8
E, HID = 3, 512
HC = HID // P
NM = E * HC
TB = 64
NB = T // TB
N = B * TB
C = 4
NC = TB // C
CC = N // C
EPS = 1e-5
ZL = 3
PAIRS = (0, C - 1, 2 * C - 3)
QPAIRS = (0, C, 2 * C - 1, 3 * C - 3)
NPAIR, NQPAIR = C * (C - 1) // 2, C * (C + 1) // 2
QSPLIT = QPAIRS[2]
KH, FC, WW, QT, U0 = 3, 4, 5, 6, 7


def macaron_kernel(nc, x, Wq, Wk, Wv, Wgamma, Wf1, Wf2, Wog1, Wog2, norm_w, Wo,
                   gate_w, w1, b1, w2, b2, sw1, sb1, sw2, sb2, out):
    kfw_dram = nc.dram_tensor("kfw_dram", [NB, P, 3, B, TB], F32).ap()
    qu_dram = nc.dram_tensor("qu_dram", [NB, P, 2, B, TB], F32).ap()

    with ExitStack() as ctx:
        def sb(name, shape):
            return ctx.enter_context(nc.sbuf_tensor(name, [P] + shape, F32))

        def sem(name):
            return ctx.enter_context(nc.semaphore(name))

        ident = sb("ident", [P])
        center = sb("center", [P])
        average = sb("average", [P])
        heads = sb("heads", [P])
        w1_sb = sb("w1_sb", [E, HID])
        w2_sb = sb("w2_sb", [NM, D])
        b1_sb = sb("b1_sb", [NM])
        b2_sb = sb("b2_sb", [E])
        hb2 = sb("hb2", [1])
        gate_sb = sb("gate_sb", [2])
        gate_diff = sb("gate_diff", [1])
        gate_bc = sb("gate_bc", [P])
        wq_sb, wk_sb, wv_sb, wo_sb = (sb(n, [D]) for n in ("wq_sb", "wk_sb", "wv_sb", "wo_sb"))
        wgam_sb = sb("wgam_sb", [H])
        wgam_bc = sb("wgam_bc", [H, HD])
        wfo_sb = sb("wfo_sb", [2 * HD])
        wf2_sb = sb("wf2_sb", [D])
        wog2_sb = sb("wog2_sb", [D])
        nw_sb = sb("nw_sb", [1])

        x_in = sb("x_in", [2, D])
        xT = sb("xT", [N])
        sq = sb("sq", [N])
        cen = sb("cen", [N])
        eps = sb("eps", [1])
        sd = sb("sd", [2])
        rsd = sb("rsd", [2])
        xn1, xn2, xnB, onT = (sb(n, [N]) for n in ("xn1", "xn2", "xnB", "onT"))
        m0_1, m1_1, m0_2, m1_2 = (sb(n, [N]) for n in ("m0_1", "m1_1", "m0_2", "m1_2"))
        hid = sb("hid", [4, N])
        y1T = sb("y1T", [NB, N])
        y2T = sb("y2T", [N])
        y3T = sb("y3T", [N])
        og = sb("og", [NB, N])
        sig_k, sig_q, sig_g, f = (sb(n, [N]) for n in ("sig_k", "sig_q", "sig_g", "f"))
        k_raw, k_sq, q, fo, ag, a = (sb(n, [N]) for n in ("k_raw", "k_sq", "q", "fo", "ag", "a"))
        k_wide = sb("k_wide", [2, P])
        k_floor, k_len, k_inv = (sb(n, [2, H]) for n in ("k_floor", "k_len", "k_inv"))
        feat = sb("feat", [8, N])
        ap_ = sb("ap_", [NPAIR, CC])
        qp = sb("qp", [NB, NQPAIR, CC])
        solve = sb("solve", [(C - 1) * 2 * CC])
        uo_f = sb("uo_f", [2, N])
        mix = sb("mix", [C * CC])
        o_g = sb("o_g", [N])
        y_out = sb("y_out", [2, D])

        l_kfw = sb("l_kfw", [HD, 3, TB])
        l_q = sb("l_q", [HD, TB])
        l_u0 = sb("l_u0", [HD // 2, TB])
        prod = sb("prod", [TB, HD // 2, HD + 1])
        u_l = sb("u_l", [HD // 2, TB])
        outer = sb("outer", [2, HD, HD // 2, C + 1])
        state = sb("state", [NC + 1, HD, HD // 2])
        oprod = sb("oprod", [TB, HD // 2, HD])
        uo_l = sb("uo_l", [HD // 2, 2, TB])

        bank = [ctx.enter_context(nc.psum_tensor(f"bank{i}", [P, 512], F32)) for i in range(8)]
        left, right = (lambda i: bank[i][:, 0:N]), (lambda i: bank[i][:, N:2 * N])
        p_hid = [(left, right)[m % 2](m // 2) for m in range(4)]
        p_acc = left(2)
        p_cen, p_var, p_scale = left(3), bank[3][:, 0:2], left(3)
        p_qk0, p_k, p_q = bank[4][:, 0:QSPLIT * CC], left(4), right(4)
        p_qk1, p_g, p_fo, p_a = (bank[5][:, 0:(NQPAIR - QSPLIT) * CC], left(5), bank[5][0:2 * HD, N:2 * N],
                                 bank[5][:, 0:NPAIR * CC])
        p_out, p_z2, p_v, p_n, p_kscale = left(6), left(6), left(6), bank[6][:, 0:2 * H], left(6)
        p_wo, p_x, p_f, p_og, p_z1 = left(7), left(7), left(7), right(7), left(7)

        S = {}
        for name in ("w_first", "w_ffn", "w_attn", "x_in", "feat_stored", "kfw_in", "u0_in", "lq_in", "uo_back", "y_stored",
                     "consts_pool", "consts_dve", "consts_fold", "w2_half", "setup", "setup_p", "fo_zero",
                     "xT_ps", "xT_sb", "z_ps1", "z_ps2", "m1_1", "m1_2", "m0_1", "m0_2",
                     "up1", "up2", "relu1", "relu2", "down1", "down2", "acc1", "acc2",
                     "y1", "y2", "y3",
                     "cenA", "cenB", "cenC", "cenD", "sqA", "sqB", "sqC", "sqD",
                     "varA", "varB", "varC", "varD", "csA", "csB", "csC", "csD",
                     "sdA", "sdB", "sdC", "sdD", "rsA", "rsB", "rsC", "rsD", "bcA", "bcB", "bcC", "bcD", "eps",
                     "nA", "nB", "nC", "nD",
                     "k_ps", "g_ps", "q_ps", "fo_ps", "v_ps", "f_ps", "og_ps",
                     "sig_k", "sig_g", "sig_q", "fo_sb", "v_sb", "f_sb", "fc0", "og_sb",
                     "k_raw", "q_sb", "k_sq", "n_ps", "k_floor", "k_len", "k_inv", "k_wide", "k_scale", "kn", "ag", "a_sb", "fc", "wt", "qt",
                     "rr", "ap", "qp", "a_ps", "fs_mul", "fs_add",
                     "u0_lane", "s0", "carried", "c_prod", "c_decay", "c_u", "c_outer", "c_state",
                     "oprod", "o_lane", "u_lane", "qk_ps", "mix_mul", "mix_add", "o_g", "wo_ps", "out_ps", "y_out"):
            S[name] = sem(name)

        def some(count):
            return not isinstance(count, int) or count > 0

        block = ctx.enter_context(nc.Block())

        def parts(n):
            return n < NB, 1 <= n <= NB, ZL <= n < NB + ZL, n >= ZL + 1, 2 <= n < NB + 2, n + 1 < NB

        STEADY = (ZL + 1, NB - 1)
        LAST = NB + ZL

        def run(eng, body):
            for n in range(STEADY[0]):
                body(n, *parts(n))
            with eng.Fori(STEADY[0], STEADY[1]) as n:
                body(n, *[True] * 6)
            for n in range(STEADY[1], LAST + 1):
                body(n, *parts(n))

        ORDER = (2, 1, 0)

        def at_most(n, top):
            return min(n, top) if isinstance(n, int) else n

        SLOTS = [("up", 0), ("up", 1)]
        for m in range(0, NM, 2):
            SLOTS += [("up", m + 2), ("up", m + 3)] if m + 2 < NM else []
            SLOTS += [("down", m), ("down", m + 1)]

        def ups(slots):
            return sum(kind == "up" for kind, _ in SLOTS[:slots]) // 2 * 2

        def steps(t, cc=CC):
            return t.rearrange("p (c j) -> p j c", j=C)

        featf = feat[:, :, :].rearrange("p a n -> p (a n)")
        key_diag = featf[:, 0:C * (N + 1)].rearrange("p (j r) -> p j r", r=N + 1)[:, :, 0:N - C + 1:C]
        keys = feat[:, 0:C, :].rearrange("p j (c s) -> p j c s", s=C)
        uw = feat[:, WW:U0 + 1:U0 - WW, :].rearrange("p x (c j) -> p x c j", j=C)

        @block.sync
        def _(sp):
            def load_x(n):
                for half in range(2):
                    src = x[2 * half:2 * half + 2, bass.ds(n * TB, TB), :]
                    sp.dma_start(x_in[:, half, :], src).then_inc(S["x_in"], 16)

            load_x(0)
            sp.dma_start(gate_sb[:, :], gate_w.rearrange("e d -> d e"), allow_slow_non_contiguous=True).then_inc(S["w_first"], 16)
            sp.dma_start(w1_sb[:, 0:2, :], w1.rearrange("e d h -> d e h")).then_inc(S["w_ffn"], 16)
            sp.dma_start(w1_sb[:, 2, :], sw1).then_inc(S["w_ffn"], 16)
            sp.dma_start(b1_sb[:, 0:2 * HC], b1.rearrange("e (c p) -> p (e c)", p=P), allow_slow_non_contiguous=True).then_inc(S["w_ffn"], 16)
            sp.dma_start(b1_sb[:, 2 * HC:NM], sb1.rearrange("(c p) -> p c", p=P), allow_slow_non_contiguous=True).then_inc(S["w_ffn"], 16)
            sp.dma_start(w2_sb[:, 0:2 * HC, :], w2.rearrange("e (c p) d -> p (e c) d", p=P)).then_inc(S["w_ffn"], 16)
            sp.dma_start(w2_sb[:, 2 * HC:NM, :], sw2.rearrange("(c p) d -> p c d", p=P)).then_inc(S["w_ffn"], 16)
            sp.dma_start(b2_sb[:, 0:2], b2.rearrange("e d -> d e"), allow_slow_non_contiguous=True).then_inc(S["w_ffn"], 16)
            sp.dma_start(b2_sb[:, 2:3], sb2.rearrange("(d a) -> d a", a=1), allow_slow_non_contiguous=True).then_inc(S["w_ffn"], 16)
            for dst, src in ((wq_sb, Wq), (wk_sb, Wk), (wv_sb, Wv), (wo_sb, Wo), (wgam_sb, Wgamma)):
                sp.dma_start(dst[:, :], src).then_inc(S["w_attn"], 16)
            sp.dma_start(wfo_sb[:, 0:HD], Wf1).then_inc(S["w_attn"], 16)
            sp.dma_start(wfo_sb[:, HD:2 * HD], Wog1).then_inc(S["w_attn"], 16)
            sp.wait_ge(S["fo_zero"], 2)
            sp.dma_start(wf2_sb[0:HD, :], Wf2).then_inc(S["w_attn"], 16)
            sp.dma_start(wog2_sb[HD:2 * HD, :], Wog2).then_inc(S["w_attn"], 16)
            sp.dma_start(nw_sb[:, :], norm_w.rearrange("(d a) -> d a", a=1), allow_slow_non_contiguous=True).then_inc(S["w_attn"], 16)

            def body(n, first, scan, second, store, back, more):
                if more:
                    sp.wait_ge(S["xT_ps"], n + 1)
                    load_x(n + 1)
                if store:
                    t = n - ZL - 1
                    sp.wait_ge(S["y_out"], t + 1)
                    for half in range(2):
                        sp.dma_start(out[2 * half:2 * half + 2, bass.ds(t * TB, TB), :],
                                     y_out[:, half, :]).then_inc(S["y_stored"], 16)
                if back:
                    d = n - 2
                    sp.wait_ge(S["u_lane"], d + 1)
                    sp.wait_ge(S["o_lane"], d + 1)
                    if some(C * d):
                        sp.wait_ge(S["mix_add"], C * d)
                    if some(d):
                        sp.wait_ge(S["o_g"], d)
                    for vh in range(2):
                        for b in range(B):
                            sp.dma_start(uo_f[vh:P:2, :, TB * b:TB * b + TB],
                                         uo_l[64 * vh + H * b:64 * vh + H * b + H, :, :, :]).then_inc(S["uo_back"], 16)
                if first:
                    sp.wait_ge(S["fs_add"], 3 * (n + 1))
                    sp.wait_ge(S["qt"], n + 1)
                    sp.wait_ge(S["rr"], 3 * (n + 1))
                    sp.dma_start(kfw_dram[n].rearrange("p a b t -> p (a b t)"),
                                 feat[:, KH:WW + 1, :]).then_inc(S["feat_stored"], 16)
                    sp.dma_start(qu_dram[n].rearrange("p a b t -> p (a b t)"),
                                 feat[:, QT:U0 + 1, :]).then_inc(S["feat_stored"], 16)
                    sp.wait_ge(S["feat_stored"], 32 * (n + 1))
                    if some(NC * n):
                        sp.wait_ge(S["c_state"], NC * n)
                    for vh in range(2):
                        sp.dma_start(l_kfw[64 * vh:64 * vh + 64, :, :, :],
                                     kfw_dram[n].rearrange("(h k) a b t -> b h k a t", k=HD))\
                          .then_inc(S["kfw_in"], 16)
                    if some(n):
                        sp.wait_ge(S["u0_lane"], n)
                    for vh in range(2):
                        sp.dma_start(l_u0[64 * vh:64 * vh + 64, :, :],
                                     qu_dram[n][:, 1].rearrange("(h v g) b t -> g b h v t", v=HD // 2, g=2)[vh])\
                          .then_inc(S["u0_in"], 16)
                    if some(C * n):
                        sp.wait_ge(S["oprod"], C * n)
                    for vh in range(2):
                        sp.dma_start(l_q[64 * vh:64 * vh + 64, :, :],
                                     qu_dram[n][:, 0].rearrange("(h k) b t -> b h k t", k=HD))\
                          .then_inc(S["lq_in"], 16)
            for n in range(LAST + 1):
                body(n, *parts(n))
            sp.wait_ge(S["y_stored"], 32 * NB + 1)

        @block.tensor
        def _(pe):
            mm = nc.tensor.matmul

            def slot(tag, b, i):
                kind, m = SLOTS[i]
                e, w = ORDER[m // HC], ORDER[m // HC] * HC + m % HC
                if kind == "up":
                    if m == 0:
                        pe.wait_ge(S[("nA", "nD")[tag - 1]], b + 1)
                    if m == HC:
                        pe.wait_ge(S[f"m1_{tag}"], b + 1)
                    if m == 2 * HC:
                        pe.wait_ge(S[f"m0_{tag}"], b + 1)
                    if m in (0, 2):
                        other = (b - ZL, at_most(b + ZL + 1, NB))[tag - 1]
                        if some(NM * other - 2 + m):
                            pe.wait_ge(S[f"relu{3 - tag}"], NM * other - 2 + m)
                    if m % 2 == 0:
                        if some(NM * b + m - 2):
                            pe.wait_ge(S[f"relu{tag}"], NM * b + m - 2)
                    src = {2: (xn1, xn2), 1: (m1_1, m1_2), 0: (m0_1, m0_2)}[e][tag - 1]
                    mm(p_hid[m % 4], w1_sb[:, e, P * (m % HC):P * (m % HC) + P], src[:, :],
                       start=True, stop=True).then_inc(S[f"up{tag}"], 1)
                else:
                    if m == 0:
                        if some(b):
                            pe.wait_ge(S[("y1", "y3")[tag - 1]], b)
                        if some((b - ZL, at_most(b + ZL + 1, NB))[tag - 1]):
                            pe.wait_ge(S[("y3", "y1")[tag - 1]], (b - ZL, at_most(b + ZL + 1, NB))[tag - 1])
                    pe.wait_ge(S[f"relu{tag}"], NM * b + m + 1)
                    mm(p_acc, w2_sb[:, w, :], hid[:, m % 4, :], start=m == 0, stop=m == NM - 1)\
                        .then_inc(S[f"down{tag}"], 1)

            def ffn(tag, b, lo, hi, there):
                if there:
                    for i in range(lo, hi):
                        slot(tag, b, i)

            def transposed_in(b):
                pe.wait_ge(S["x_in"], 32 * (b + 1))
                if some(b):
                    pe.wait_ge(S["m1_1"], b)
                for half in range(2):
                    last = nc.tensor.transpose(p_x[:, P * half:P * half + P], x_in[:, half, :], ident[:, :])
                last.then_inc(S["xT_ps"], 1)

            def centered(tag, b, src, ready):
                pe.wait_ge(S[ready], b + 1)
                mm(p_cen, center[:, :], src, start=True, stop=True).then_inc(S["cen" + tag], 1)

            def variance(tag, b):
                pe.wait_ge(S["sq" + tag], b + 1)
                pe.wait_ge(S["cs" + tag], b + 1)
                for half in range(2):
                    last = mm(p_var[:, half:half + 1], sq[:, P * half:P * half + P], average[:, 0:1], start=True, stop=True)
                last.then_inc(S["var" + tag], 1)

            def spread(tag, b):
                pe.wait_ge(S["rs" + tag], b + 1)
                for half in range(2):
                    last = mm(p_scale[:, P * half:P * half + P], rsd[:, half:half + 1].to_broadcast([P, P]), ident[:, :],
                              start=True, stop=True)
                last.then_inc(S["bc" + tag], 1)

            def routed(tag, b, src):
                pe.wait_ge(S[("nA", "nD")[tag - 1]], b + 1)
                mm((p_z1, p_z2)[tag - 1], gate_bc[:, :], src[:, :], start=True, stop=True).then_inc(S[f"z_ps{tag}"], 1)

            pe.wait_ge(S["setup_p"], 3)
            pe.wait_ge(S["setup"], 5)
            pe.wait_ge(S["w_ffn"], 16 * 8)
            pe.wait_ge(S["w_attn"], 16 * 10)
            transposed_in(0)
            centered("A", 0, xT[:, :], "xT_sb")
            variance("A", 0)
            spread("A", 0)
            routed(1, 0, xn1)

            def body(n, first, scan, second, store, back, more):
                z, t = n - ZL, n - ZL - 1
                if second:
                    pe.wait_ge(S["qp"], C * (z + 1))
                    if some(at_most(n, NB)):
                        pe.wait_ge(S["q_sb"], at_most(n, NB))
                    if some(3 * at_most(n, NB)):
                        pe.wait_ge(S["fs_mul"], 3 * at_most(n, NB))
                    if some(C * z):
                        pe.wait_ge(S["mix_mul"], C * z)
                    mm(p_qk0, heads[:, :], qp[:, z, 0:QSPLIT, :], start=True, stop=True)
                    mm(p_qk1, heads[:, :], qp[:, z, QSPLIT:NQPAIR, :], start=True, stop=True).then_inc(S["qk_ps"], 1)
                ffn(1, n, 0, 4, first)
                if store:
                    pe.wait_ge(S["y3"], t + 1)
                    if some(at_most(n, NB)):
                        pe.wait_ge(S["kn"], at_most(n, NB))
                    if some(at_most(z, NB)):
                        pe.wait_ge(S["m1_2"], at_most(z, NB))
                    for half in range(2):
                        last = nc.tensor.transpose(p_out[:, P * half:P * half + P], y3T[:, P * half:P * half + P], ident[:, :])
                    last.then_inc(S["out_ps"], 1)
                ffn(1, n, 4, 10, first)
                if second:
                    pe.wait_ge(S["nA"], at_most(n + 1, NB))
                    if some(z):
                        pe.wait_ge(S["nD"], z)
                    centered("C", z, o_g[:, :], "o_g")
                ffn(1, n, 10, 12, first)
                if second:
                    variance("C", z)
                ffn(1, n, 12, 15, first)
                if second:
                    spread("C", z)
                ffn(1, n, 15, 17, first)
                if second:
                    pe.wait_ge(S["nC"], z + 1)
                    pe.wait_ge(S["m1_1"], at_most(n + 1, NB))
                    if some(z):
                        pe.wait_ge(S["y2"], z)
                    mm(p_wo, wo_sb[:, :], onT[:, :], start=True, stop=True).then_inc(S["wo_ps"], 1)
                ffn(1, n, 17, 19, first)
                if second:
                    centered("D", z, y2T[:, :], "y2")
                ffn(1, n, 19, 21, first)
                if second:
                    variance("D", z)
                ffn(1, n, 21, 24, first)
                if second:
                    spread("D", z)

                ffn(2, z, 0, 1, second)
                if second:
                    if some(z):
                        pe.wait_ge(S["y_out"], z)
                    if some(at_most(n, NB)):
                        pe.wait_ge(S["kn"], at_most(n, NB))
                    routed(2, z, xn2)
                ffn(2, z, 1, 3, second)
                if first:
                    pe.wait_ge(S["nA"], n + 1)
                    if second:
                        pe.wait_ge(S["nD"], z + 1)
                    centered("B", n, y1T[:, n, :], "y1")
                if more:
                    if second:
                        pe.wait_ge(S["y2"], z + 1)
                    transposed_in(n + 1)
                ffn(2, z, 3, 5, second)
                if first:
                    variance("B", n)
                ffn(2, z, 5, 8, second)
                if first:
                    spread("B", n)
                ffn(2, z, 8, 10, second)
                if first:
                    pe.wait_ge(S["nB"], n + 1)
                    if some(3 * n):
                        pe.wait_ge(S["fs_mul"], 3 * n)
                    if second:
                        pe.wait_ge(S["mix_mul"], C * (z + 1))
                    mm(p_g, wgam_bc[:, :, :], xnB[:, :], start=True, stop=True).then_inc(S["g_ps"], 1)
                    mm(p_fo, wfo_sb[:, :], xnB[:, :], start=True, stop=True).then_inc(S["fo_ps"], 1)
                    if some(n):
                        pe.wait_ge(S["q_sb"], n)
                    mm(p_k, wk_sb[:, :], xnB[:, :], start=True, stop=True).then_inc(S["k_ps"], 1)
                    mm(p_q, wq_sb[:, :], xnB[:, :], start=True, stop=True).then_inc(S["q_ps"], 1)
                    if some(n):
                        pe.wait_ge(S["kn"], n)
                    if second:
                        pe.wait_ge(S["m1_2"], z + 1)
                    mm(p_v, wv_sb[:, :], xnB[:, :], start=True, stop=True).then_inc(S["v_ps"], 1)
                    pe.wait_ge(S["fo_sb"], n + 1)
                    pe.wait_ge(S["m1_1"], n + 1)
                    if second:
                        pe.wait_ge(S["y2"], z + 1)
                    if more:
                        pe.wait_ge(S["xT_sb"], n + 2)
                    mm(p_f, wf2_sb[0:2 * HD, :], fo[0:2 * HD, :], start=True, stop=True).then_inc(S["f_ps"], 1)
                    mm(p_og, wog2_sb[0:2 * HD, :], fo[0:2 * HD, :], start=True, stop=True).then_inc(S["og_ps"], 1)
                ffn(2, z, 10, 12, second)
                if more:
                    pe.wait_ge(S["nB"], n + 1)
                    centered("A", n + 1, xT[:, :], "xT_sb")
                ffn(2, z, 12, 13, second)
                if first:
                    pe.wait_ge(S["k_sq"], n + 1)
                    pe.wait_ge(S["v_sb"], n + 1)
                    for half in range(2):
                        last = mm(p_n[:, H * half:H * half + H], k_sq[:, P * half:P * half + P], heads[:, 0:P:HD],
                                  start=True, stop=True)
                    last.then_inc(S["n_ps"], 1)
                ffn(2, z, 13, 15, second)
                if more:
                    variance("A", n + 1)
                if first:
                    pe.wait_ge(S["k_wide"], n + 1)
                    for half in range(2):
                        last = mm(p_kscale[:, P * half:P * half + P],
                                  k_wide[:, half, :], ident[:, :], start=True, stop=True)
                    last.then_inc(S["k_scale"], 1)
                ffn(2, z, 15, 18, second)
                if more:
                    spread("A", n + 1)
                ffn(2, z, 18, 20, second)
                if more:
                    pe.wait_ge(S["og_sb"], n + 1)
                    routed(1, n + 1, xn1)
                ffn(2, z, 20, 24, second)
                if first:
                    pe.wait_ge(S["ap"], 3 * (n + 1))
                    pe.wait_ge(S["fo_sb"], n + 1)
                    pe.wait_ge(S["sig_g"], n + 1)
                    mm(p_a, heads[:, :], ap_[:, :, :], start=True, stop=True).then_inc(S["a_ps"], 1)
            run(pe, body)

        @block.scalar
        def _(act):
            def relu(tag, b, lo, hi, there):
                if there:
                    for m in range(ups(lo), ups(hi)):
                        w = ORDER[m // HC] * HC + m % HC
                        act.wait_ge(S[f"up{tag}"], NM * b + m // 2 * 2 + 2)
                        if m < 4:
                            other = (b - ZL, at_most(b + ZL + 1, NB))[tag - 1]
                            if some(NM * other - 3 + m):
                                act.wait_ge(S[f"down{3 - tag}"], NM * other - 3 + m)
                        if some(NM * b + m - 3):
                            act.wait_ge(S[f"down{tag}"], NM * b + m - 3)
                        nc.scalar.activation(hid[:, m % 4, :], p_hid[m % 4], ACT.Relu, bias=b1_sb[:, w:w + 1])\
                            .then_inc(S[f"relu{tag}"], 1)

            def centred(tag, b):
                act.wait_ge(S["cen" + tag], b + 1)
                nc.scalar.activation(sq[:, :], p_cen, ACT.Square).then_inc(S["sq" + tag], 1)
                nc.scalar.copy(cen[:, :], p_cen).then_inc(S["cs" + tag], 1)

            def deviation(tag, b):
                act.wait_ge(S["var" + tag], b + 1)
                nc.scalar.activation(sd[:, :], p_var, ACT.Sqrt, bias=eps[:, :]).then_inc(S["sd" + tag], 1)

            def x_copy(b):
                act.wait_ge(S["xT_ps"], b + 1)
                if some(b):
                    act.wait_ge(S["y1"], b)
                nc.scalar.copy(xT[:, :], p_x).then_inc(S["xT_sb"], 1)

            act.wait_ge(S["w_ffn"], 16 * 8)
            act.wait_ge(S["eps"], 1)
            x_copy(0)
            centred("A", 0)
            deviation("A", 0)

            def body(n, first, scan, second, store, back, more):
                z, t = n - ZL, n - ZL - 1
                relu(1, n, 0, 4, first)
                if store:
                    act.wait_ge(S["out_ps"], t + 1)
                    act.wait_ge(S["y_stored"], 32 * t + 1)
                    nc.scalar.copy(y_out[:, :, :], p_out.rearrange("p (h d) -> p h d", h=2)).then_inc(S["y_out"], 1)
                relu(1, n, 4, 10, first)
                if second:
                    act.wait_ge(S["nA"], at_most(n + 1, NB))
                    if some(z):
                        act.wait_ge(S["nD"], z)
                    centred("C", z)
                relu(1, n, 10, 12, first)
                if second:
                    deviation("C", z)
                relu(1, n, 12, 19, first)
                if second:
                    act.wait_ge(S["nC"], z + 1)
                    centred("D", z)
                relu(1, n, 19, 21, first)
                if second:
                    deviation("D", z)
                relu(1, n, 21, 24, first)

                relu(2, z, 0, 3, second)
                if first:
                    act.wait_ge(S["nA"], n + 1)
                    if second:
                        act.wait_ge(S["nD"], z + 1)
                    centred("B", n)
                if more:
                    x_copy(n + 1)
                relu(2, z, 3, 5, second)
                if first:
                    deviation("B", n)
                relu(2, z, 5, 10, second)
                if first:
                    act.wait_ge(S["fo_ps"], n + 1)
                    nc.scalar.copy(fo[0:2 * HD, :], p_fo).then_inc(S["fo_sb"], 1)
                    if some(n):
                        act.wait_ge(S["ag"], n)
                    nc.scalar.activation(sig_g[:, :], p_g, ACT.Sigmoid).then_inc(S["sig_g"], 1)
                    act.wait_ge(S["q_ps"], n + 1)
                    if some(n):
                        act.wait_ge(S["k_raw"], n)
                    nc.scalar.activation(sig_k[:, :], p_k, ACT.Sigmoid).then_inc(S["sig_k"], 1)
                    if some(n):
                        act.wait_ge(S["q_sb"], n)
                    nc.scalar.activation(sig_q[:, :], p_q, ACT.Sigmoid).then_inc(S["sig_q"], 1)
                    act.wait_ge(S["v_ps"], n + 1)
                    if some(32 * n):
                        act.wait_ge(S["feat_stored"], 32 * n)
                    nc.scalar.copy(feat[:, U0, :], p_v).then_inc(S["v_sb"], 1)
                    act.wait_ge(S["og_ps"], n + 1)
                    if some(3 * n):
                        act.wait_ge(S["rr"], 3 * n)
                    if some(n):
                        act.wait_ge(S["a_sb"], n)
                    nc.scalar.activation(f[:, :], p_f, ACT.Sigmoid).then_inc(S["f_sb"], 1)
                    nc.scalar.activation(steps(feat[:, FC, :])[:, 0], steps(p_f)[:, 0], ACT.Sigmoid).then_inc(S["fc0"], 1)
                    nc.scalar.activation(og[:, n, :], p_og, ACT.Sigmoid).then_inc(S["og_sb"], 1)
                    act.wait_ge(S["k_raw"], n + 1)
                    nc.scalar.activation(k_sq[:, :], k_raw[:, :], ACT.Square).then_inc(S["k_sq"], 1)
                relu(2, z, 10, 12, second)
                if more:
                    act.wait_ge(S["nB"], n + 1)
                    centred("A", n + 1)
                relu(2, z, 12, 13, second)
                if first:
                    act.wait_ge(S["k_floor"], n + 1)
                    nc.scalar.activation(k_len[:, :, :], k_floor[:, :, :], ACT.Sqrt).then_inc(S["k_len"], 1)
                    act.wait_ge(S["k_inv"], n + 1)
                    nc.scalar.copy(k_wide[:, :, :].rearrange("p a (h k) -> p a h k", k=HD),
                                   k_inv[:, :, :, None].to_broadcast([P, 2, H, HD])).then_inc(S["k_wide"], 1)
                relu(2, z, 13, 15, second)
                if more:
                    deviation("A", n + 1)
                relu(2, z, 15, 24, second)
            run(act, body)

        @block.vector
        def _(dve):
            tt, ts, stt = nc.vector.tensor_tensor, nc.vector.tensor_scalar, nc.vector.scalar_tensor_tensor

            nc.vector.memset(wf2_sb[0:2 * HD, :], 0.0).then_inc(S["fo_zero"], 1)
            nc.vector.memset(wog2_sb[0:2 * HD, :], 0.0).then_inc(S["fo_zero"], 1)
            nc.vector.memset(eps[:, :], EPS).then_inc(S["eps"], 1)
            nc.vector.memset(y_out[:, :, :], 0.0).then_inc(S["y_stored"], 1)
            nc.vector.memset(state[:, NC, :, :], 0.0).then_inc(S["s0"], 1)
            dve.wait_ge(S["w_first"], 16)
            tt(gate_diff[:, :], gate_sb[:, 1:2], gate_sb[:, 0:1], ALU.subtract).then_inc(S["consts_dve"], 1)
            dve.wait_ge(S["consts_dve"], 1)
            dve.wait_ge(S["consts_pool"], 2)
            ts(gate_bc[:, :], average[:, :], 0.0, gate_diff[:, :], ALU.mult, ALU.add).then_inc(S["setup"], 1)
            dve.wait_ge(S["w_ffn"], 16 * 8)
            nc.vector.tensor_reduce(hb2[:, :], b2_sb[:, :], axis=AX.X, op=ALU.add).then_inc(S["consts_dve"], 1)
            ts(w2_sb[:, :, :], w2_sb[:, :, :], 0.5, None, ALU.mult).then_inc(S["setup"], 1)
            dve.wait_ge(S["consts_dve"], 2)
            ts(hb2[:, :], hb2[:, :], 0.5, None, ALU.mult).then_inc(S["setup"], 1)
            dve.wait_ge(S["w_attn"], 16 * 10)
            ts(wo_sb[:, :], wo_sb[:, :], nw_sb[:, :], None, ALU.mult).then_inc(S["setup"], 1)
            nc.vector.tensor_copy(wgam_bc[:, :, :], wgam_sb[:, :, None].to_broadcast([P, H, HD])).then_inc(S["setup"], 1)
            dve.wait_ge(S["setup"], 5)

            def inverse_deviation(tag, b):
                dve.wait_ge(S["sd" + tag], b + 1)
                nc.vector.reciprocal(rsd[:, :], sd[:, :]).then_inc(S["rs" + tag], 1)

            def normalised(tag, b, dst):
                dve.wait_ge(S["bc" + tag], b + 1)
                dve.wait_ge(S["cs" + tag], b + 1)
                tt(dst[:, :], cen[:, :], p_scale, ALU.mult).then_inc(S["n" + tag], 1)

            def routing(tag, b, src, dst):
                dve.wait_ge(S[f"z_ps{tag}"], b + 1)
                stt(dst[:, :], (p_z1, p_z2)[tag - 1], 0.0, src[:, :], ALU.is_gt, ALU.mult).then_inc(S[f"m1_{tag}"], 1)

            inverse_deviation("A", 0)
            normalised("A", 0, xn1)
            routing(1, 0, xn1, m1_1)

            def scan_op(b, i):
                c, kind = divmod(i, 5)
                done = NC * b + c
                steps_c = slice(C * c, C * c + C)
                now, nxt = c, c + 1
                if kind == 0:
                    if c == 0:
                        dve.wait_ge(S["u0_in"], 32 * (b + 1))
                        if some(done):
                            dve.wait_ge(S["c_u"], done)
                        nc.vector.tensor_copy(prod[:, :, :, HD], l_u0[:, :, :].rearrange("p v t -> p t v"))\
                            .then_inc(S["u0_lane"], 1)
                        if some(C * b):
                            dve.wait_ge(S["oprod"], C * b)
                        if some(done):
                            dve.wait_ge(S["c_state"], done)
                        dve.wait_ge(S["s0"], 1)
                        nc.vector.tensor_copy(state[:, 0], state[:, NC]).then_inc(S["carried"], 1)
                        dve.wait_ge(S["carried"], b + 1)
                        dve.wait_ge(S["kfw_in"], 32 * (b + 1))
                    if some(done):
                        dve.wait_ge(S["c_state"], done)
                    tt(prod[:, steps_c, :, 0:HD],
                       l_kfw[:, :, 2, steps_c].rearrange("p k j -> p j k")[:, :, None, :].to_broadcast([P, C, HD // 2, HD]),
                       state[:, now].rearrange("p k v -> p v k")[:, None].to_broadcast([P, C, HD // 2, HD]),
                       ALU.mult).then_inc(S["c_prod"], 1)
                elif kind == 1:
                    tt(outer[:, c % 2, :, :, C],
                       l_kfw[:, :, 1, C * c + C - 1][:, :, None].to_broadcast([P, HD, HD // 2]),
                       state[:, now], ALU.mult).then_inc(S["c_decay"], 1)
                elif kind == 2:
                    if c == 0:
                        dve.wait_ge(S["u0_lane"], b + 1)
                        if some(b):
                            dve.wait_ge(S["u_lane"], b)
                    dve.wait_ge(S["c_prod"], done + 1)
                    nc.vector.tensor_reduce(u_l[:, :, steps_c].rearrange("p v j -> p j v"), prod[:, steps_c],
                                            axis=AX.X, op=ALU.add).then_inc(S["c_u"], 1)
                elif kind == 3:
                    dve.wait_ge(S["c_u"], done + 1)
                    tt(outer[:, c % 2, :, :, 0:C],
                       l_kfw[:, :, 0, steps_c][:, :, None, :].to_broadcast([P, HD, HD // 2, C]),
                       u_l[:, :, steps_c][:, None].to_broadcast([P, HD, HD // 2, C]),
                       ALU.mult).then_inc(S["c_outer"], 1)
                else:
                    dve.wait_ge(S["c_decay"], done + 1)
                    dve.wait_ge(S["c_outer"], done + 1)
                    nc.vector.tensor_reduce(state[:, nxt], outer[:, c % 2], axis=AX.X, op=ALU.add)\
                        .then_inc(S["c_state"], 1)

            def scan(b, lo, hi, there):
                if there:
                    for i in range(lo, hi):
                        scan_op(b, i)

            def body(n, first, scanned, second, store, back, more):
                c, z = n - 1, n - ZL
                if second:
                    dve.wait_ge(S["qk_ps"], z + 1)
                    dve.wait_ge(S["uo_back"], 16 * 8 * (z + 1))
                    for s in range(C):
                        width = (C - s) * CC
                        pair = (p_qk0 if s < 2 else p_qk1)
                        at = (QPAIRS[s] - (0 if s < 2 else QSPLIT)) * CC
                        if some(C * z + s):
                            dve.wait_ge(S["mix_add"], C * z + s)
                        tt(mix[:, 0:width].rearrange("p (j c) -> p j c", c=CC),
                           pair[:, at:at + width].rearrange("p (j c) -> p j c", c=CC),
                           steps(uo_f[:, 0, :])[:, s][:, None].to_broadcast([P, C - s, CC]), ALU.mult).then_inc(S["mix_mul"], 1)
                        dve.wait_ge(S["mix_mul"], C * z + s + 1)
                        tt(steps(uo_f[:, 1, :])[:, s:C], mix[:, 0:width].rearrange("p (j c) -> p j c", c=CC),
                           steps(uo_f[:, 1, :])[:, s:C], ALU.add).then_inc(S["mix_add"], 1)
                scan(c, 0, 5, scanned)
                if second:
                    inverse_deviation("C", z)
                scan(c, 5, 7, scanned)
                if second:
                    normalised("C", z, onT)
                scan(c, 7, 14, scanned)
                if second:
                    dve.wait_ge(S["wo_ps"], z + 1)
                    tt(y2T[:, :], p_wo, y1T[:, z, :], ALU.add).then_inc(S["y2"], 1)
                scan(c, 14, 22, scanned)
                if second:
                    inverse_deviation("D", z)
                scan(c, 22, 24, scanned)
                if second:
                    normalised("D", z, xn2)
                scan(c, 24, 29, scanned)
                if second:
                    routing(2, z, xn2, m1_2)
                scan(c, 29, 32, scanned)
                if first:
                    dve.wait_ge(S["down1"], NM * (n + 1))
                    stt(y1T[:, n, :], p_acc, hb2[:, :], xT[:, :], ALU.add, ALU.add).then_inc(S["y1"], 1)
                scan(c, 32, 38, scanned)
                if first:
                    inverse_deviation("B", n)
                scan(c, 38, 40, scanned)
                if first:
                    normalised("B", n, xnB)
                scan(c, 40, 45, scanned)
                if first:
                    dve.wait_ge(S["sig_q"], n + 1)
                    tt(k_raw[:, :], p_k, sig_k[:, :], ALU.mult).then_inc(S["k_raw"], 1)
                    if some(n):
                        dve.wait_ge(S["qt"], n)
                    if some(C * n):
                        dve.wait_ge(S["qp"], C * n)
                    tt(q[:, :], p_q, sig_q[:, :], ALU.mult).then_inc(S["q_sb"], 1)
                scan(c, 45, 47, scanned)
                if first:
                    dve.wait_ge(S["n_ps"], n + 1)
                    ts(k_floor[:, :, :], p_n.rearrange("p (a h) -> p a h", a=2), 1e-24, None, ALU.max).then_inc(S["k_floor"], 1)
                scan(c, 47, 49, scanned)
                if first:
                    dve.wait_ge(S["k_len"], n + 1)
                    nc.vector.reciprocal(k_inv[:, :, :], k_len[:, :, :]).then_inc(S["k_inv"], 1)
                scan(c, 49, 50, scanned)
                if more:
                    inverse_deviation("A", n + 1)
                scan(c, 50, 53, scanned)
                if first:
                    dve.wait_ge(S["k_scale"], n + 1)
                    if some(C * n):
                        dve.wait_ge(S["qp"], C * n)
                    if some(32 * n):
                        dve.wait_ge(S["feat_stored"], 32 * n)
                    tt(key_diag, steps(k_raw[:, :]), steps(p_kscale), ALU.mult).then_inc(S["kn"], 1)
                scan(c, 53, 54, scanned)
                if first:
                    dve.wait_ge(S["kn"], n + 1)
                    if some(n):
                        dve.wait_ge(S["a_sb"], n)
                    stt(steps(ag[:, :]), key_diag, -1.0, steps(sig_g[:, :]), ALU.mult, ALU.mult).then_inc(S["ag"], 1)
                scan(c, 54, 56, scanned)
                if more:
                    normalised("A", n + 1, xn1)
                scan(c, 56, 61, scanned)
                if more:
                    routing(1, n + 1, xn1, m1_1)
                scan(c, 61, 66, scanned)
                if first:
                    dve.wait_ge(S["rr"], 3 * (n + 1))
                    dve.wait_ge(S["a_sb"], n + 1)
                    for s in range(C - 1):
                        tt(ap_[:, PAIRS[s]:PAIRS[s] + C - 1 - s, :], steps(a[:, :])[:, s + 1:C], keys[:, s + 1:C, :, s],
                           ALU.mult).then_inc(S["ap"], 1)
                scan(c, 66, 74, scanned)
                if first:
                    dve.wait_ge(S["a_ps"], n + 1)
                    dve.wait_ge(S["wt"], n + 1)
                    dve.wait_ge(S["v_sb"], n + 1)
                    for s in range(C - 1):
                        left = C - 1 - s
                        tmp = solve[:, 0:left * 2 * CC].rearrange("p (j x c) -> p j x c", x=2, c=CC)
                        if some(3 * n + s):
                            dve.wait_ge(S["fs_add"], 3 * n + s)
                        tt(tmp, p_a.rearrange("p (j c) -> p j c", c=CC)[:, PAIRS[s]:PAIRS[s] + left][:, :, None]
                           .to_broadcast([P, left, 2, CC]),
                           uw[:, :, :, s][:, None].to_broadcast([P, left, 2, CC]), ALU.mult).then_inc(S["fs_mul"], 1)
                        scan(c, 74 + 2 * s, 76 + 2 * s, scanned)
                        dve.wait_ge(S["fs_mul"], 3 * n + s + 1)
                        dst = uw[:, :, :, s + 1:C].rearrange("p x c j -> p j x c")
                        tt(dst, tmp, dst, ALU.add).then_inc(S["fs_add"], 1)
                else:
                    scan(c, 74, 80, scanned)
                if second:
                    dve.wait_ge(S["down2"], NM * (z + 1))
                    if some(z):
                        dve.wait_ge(S["out_ps"], z)
                    stt(y3T[:, :], p_acc, hb2[:, :], y2T[:, :], ALU.add, ALU.add).then_inc(S["y3"], 1)
                if scanned:
                    dve.wait_ge(S["c_u"], NC * (c + 1))
                    if some(16 * 8 * c):
                        dve.wait_ge(S["uo_back"], 16 * 8 * c)
                    nc.vector.tensor_copy(uo_l[:, :, 0, :], u_l[:, :, :]).then_inc(S["u_lane"], 1)
                    dve.wait_ge(S["oprod"], C * (c + 1))
                    nc.vector.tensor_reduce(uo_l[:, :, 1, :].rearrange("p v t -> p t v"), oprod[:, :, :, :],
                                            axis=AX.X, op=ALU.add).then_inc(S["o_lane"], 1)
            run(dve, body)

        @block.gpsimd
        def _(pool):
            tt = nc.gpsimd.tensor_tensor
            nc.gpsimd.memset(ident[:, :], 0.0).then_inc(S["consts_pool"], 1)
            nc.gpsimd.memset(average[:, :], 1.0 / D).then_inc(S["consts_pool"], 1)
            nc.gpsimd.memset(heads[:, :], 1.0).then_inc(S["consts_pool"], 1)
            pool.wait_ge(S["consts_pool"], 3)
            nc.gpsimd.affine_select(out=ident[:, :], in_=ident[:, :], compare_op=ALU.not_equal, fill=1.0, base=0,
                                    pattern=[[-1, P]], channel_multiplier=1).then_inc(S["setup_p"], 1)
            hv = heads[:, :].rearrange("p (h k) -> p h k", k=HD)
            nc.gpsimd.affine_select(out=hv, in_=hv, compare_op=ALU.is_ge, fill=0.0, base=0,
                                    pattern=[[-HD, H], [0, HD]], channel_multiplier=1).then_inc(S["consts_fold"], 1)
            pool.wait_ge(S["consts_fold"], 1)
            nc.gpsimd.affine_select(out=hv, in_=hv, compare_op=ALU.is_ge, fill=0.0, base=HD - 1,
                                    pattern=[[HD, H], [0, HD]], channel_multiplier=-1).then_inc(S["setup_p"], 1)
            pool.wait_ge(S["setup_p"], 2)
            tt(center[:, :], ident[:, :], average[:, :], ALU.subtract).then_inc(S["setup_p"], 1)

            def rest(tag, b, whole, one, dst):
                pool.wait_ge(S[f"m1_{tag}"], b + 1)
                tt(dst[:, :], whole[:, :], one[:, :], ALU.subtract).then_inc(S[f"m0_{tag}"], 1)

            rest(1, 0, xn1, m1_1, m0_1)

            def body(n, first, scanned, second, store, back, more):
                c, z = n - 1, n - ZL
                if second:
                    pool.wait_ge(S["mix_add"], C * (z + 1))
                    tt(o_g[:, :], uo_f[:, 1, :], og[:, z, :], ALU.mult).then_inc(S["o_g"], 1)
                    rest(2, z, xn2, m1_2, m0_2)
                if first:
                    pool.wait_ge(S["f_sb"], n + 1)
                    pool.wait_ge(S["fc0"], n + 1)
                    for j in range(1, C):
                        if some(3 * n + j - 1):
                            pool.wait_ge(S["fc"], 3 * n + j - 1)
                        tt(steps(feat[:, FC, :])[:, j], steps(feat[:, FC, :])[:, j - 1], steps(f[:, :])[:, j], ALU.mult)\
                            .then_inc(S["fc"], 1)
                    pool.wait_ge(S["q_sb"], n + 1)
                    pool.wait_ge(S["fc"], 3 * (n + 1))
                    tt(feat[:, QT, :], q[:, :], feat[:, FC, :], ALU.mult).then_inc(S["qt"], 1)
                    pool.wait_ge(S["kn"], n + 1)
                    for j in range(1, C):
                        if some(3 * n + j - 1):
                            pool.wait_ge(S["rr"], 3 * n + j - 1)
                        tt(keys[:, j, :, 0:j], keys[:, j - 1, :, 0:j],
                           steps(f[:, :])[:, j][:, :, None].to_broadcast([P, CC, j]), ALU.mult).then_inc(S["rr"], 1)
                    pool.wait_ge(S["ag"], n + 1)
                    if some(3 * n):
                        pool.wait_ge(S["ap"], 3 * n)
                    tt(a[:, :], ag[:, :], f[:, :], ALU.mult).then_inc(S["a_sb"], 1)
                    pool.wait_ge(S["a_sb"], n + 1)
                    tt(feat[:, WW, :], a[:, :], feat[:, FC, :], ALU.mult).then_inc(S["wt"], 1)
                if more:
                    rest(1, n + 1, xn1, m1_1, m0_1)
                if first:
                    pool.wait_ge(S["rr"], 3 * (n + 1))
                    for s in range(C):
                        tt(qp[:, n, QPAIRS[s]:QPAIRS[s] + C - s, :], steps(q[:, :])[:, s:C], keys[:, s:C, :, s],
                           ALU.mult).then_inc(S["qp"], 1)
                if scanned:
                    pool.wait_ge(S["lq_in"], 32 * (c + 1))
                    pool.wait_ge(S["c_state"], NC * (c + 1))
                    if some(c):
                        pool.wait_ge(S["o_lane"], c)
                    for j in range(C):
                        tt(oprod[:, j:TB:C, :, :],
                           l_q[:, :, j:TB:C].rearrange("p k c -> p c k")[:, :, None, :].to_broadcast([P, NC, HD // 2, HD]),
                           state[:, 0:NC].rearrange("p c k v -> p c v k"), ALU.mult).then_inc(S["oprod"], 1)
            run(pool, body)


_INS = ["L0_attn_x", "L0_attn_Wq", "L0_attn_Wk", "L0_attn_Wv", "L0_attn_Wgamma", "L0_attn_Wf1", "L0_attn_Wf2",
        "L0_attn_Wog1", "L0_attn_Wog2", "L0_attn_norm_w", "L0_attn_Wo", "L0_ffn_gate_w", "L0_ffn_w1", "L0_ffn_b1",
        "L0_ffn_w2", "L0_ffn_b2", "L0_ffn_sw1", "L0_ffn_sb1", "L0_ffn_sw2", "L0_ffn_sb2"]


def kernel(**inputs):
    import numpy as _np
    import concourse.bacc as _bacc
    from concourse import mybir as _mybir
    from concourse.bass_utils import run_bass_kernel_spmd as _run

    nc = _bacc.Bacc("TRN2", target_bir_lowering=False, num_devices=1)
    arrays, args = {}, []
    for name in _INS:
        a = _np.ascontiguousarray(inputs[name])
        arrays[f"in_{name}"] = a
        args.append(nc.dram_tensor(f"in_{name}", a.shape, _mybir.dt.from_np(a.dtype), kind="ExternalInput").ap())
    args.append(nc.dram_tensor("out_dram", (B, T, D), F32, kind="ExternalOutput").ap())
    macaron_kernel(nc, *args)
    r = _run(nc, [arrays], core_ids=[0])
    return r.results[0]["out_dram"]
```

```python
from contextlib import ExitStack

import concourse.bass as bass
from concourse import mybir

F32 = mybir.dt.float32
ALU = mybir.AluOpType
ACT = mybir.ActivationFunctionType
AX = mybir.AxisListType

P = 128
B, T, D = 4, 512, 128
H, HD = 16, 8
E, HID = 3, 512
HC = HID // P
NM = E * HC
TB = 64
NB = T // TB
N = B * TB
C = 4
NC = TB // C
CC = N // C
EPS = 1e-5
ZL = 3
SPLIT = 7
PAIRS = (0, C - 1, 2 * C - 3)
QPAIRS = (0, C, 2 * C - 1, 3 * C - 3)
NPAIR, NQPAIR = C * (C - 1) // 2, C * (C + 1) // 2
QSPLIT = QPAIRS[2]
KH, FC, WW, QT, U0 = 3, 4, 5, 6, 7


def macaron_kernel(nc, x, Wq, Wk, Wv, Wgamma, Wf1, Wf2, Wog1, Wog2, norm_w, Wo,
                   gate_w, w1, b1, w2, b2, sw1, sb1, sw2, sb2, out):
    kfw_dram = nc.dram_tensor("kfw_dram", [NB, P, 3, B, TB], F32).ap()
    qu_dram = nc.dram_tensor("qu_dram", [NB, P, 2, B, TB], F32).ap()

    with ExitStack() as ctx:
        def sb(name, shape):
            return ctx.enter_context(nc.sbuf_tensor(name, [P] + shape, F32))

        def sem(name):
            return ctx.enter_context(nc.semaphore(name))

        ident = sb("ident", [P])
        center = sb("center", [P])
        average = sb("average", [P])
        heads = sb("heads", [P])
        w1_sb = sb("w1_sb", [E, HID])
        w2_sb = sb("w2_sb", [NM, D])
        b1_sb = sb("b1_sb", [NM])
        b2_sb = sb("b2_sb", [E])
        hb2 = sb("hb2", [1])
        gate_sb = sb("gate_sb", [2])
        gate_diff = sb("gate_diff", [1])
        gate_bc = sb("gate_bc", [P])
        wq_sb, wk_sb, wv_sb, wo_sb = (sb(n, [D]) for n in ("wq_sb", "wk_sb", "wv_sb", "wo_sb"))
        wgam_sb = sb("wgam_sb", [H])
        wgam_bc = sb("wgam_bc", [H, HD])
        wfo_sb = sb("wfo_sb", [2 * HD])
        wf2_sb = sb("wf2_sb", [D])
        wog2_sb = sb("wog2_sb", [D])
        nw_sb = sb("nw_sb", [1])

        x_in = sb("x_in", [2, D])
        xT = sb("xT", [N])
        sq = sb("sq", [N])
        cen = sb("cen", [N])
        eps = sb("eps", [1])
        sd = sb("sd", [2])
        rsd = sb("rsd", [2])
        xn1, xn2, xnB, onT = (sb(n, [N]) for n in ("xn1", "xn2", "xnB", "onT"))
        m0_1, m1_1, m0_2, m1_2 = (sb(n, [N]) for n in ("m0_1", "m1_1", "m0_2", "m1_2"))
        hid = sb("hid", [4, N])
        y1T = sb("y1T", [NB, N])
        y2T = sb("y2T", [N])
        y3T = sb("y3T", [N])
        og = sb("og", [NB, N])
        sig_k, sig_q, sig_g, f = (sb(n, [N]) for n in ("sig_k", "sig_q", "sig_g", "f"))
        k_raw, k_sq, q, fo, ag, a = (sb(n, [N]) for n in ("k_raw", "k_sq", "q", "fo", "ag", "a"))
        k_wide = sb("k_wide", [2, P])
        k_floor, k_len, k_inv = (sb(n, [2, H]) for n in ("k_floor", "k_len", "k_inv"))
        feat = sb("feat", [8, N])
        ap_ = sb("ap_", [NPAIR, CC])
        qp = sb("qp", [NB, NQPAIR, CC])
        solve = sb("solve", [(C - 1) * 2 * CC])
        uo_f = sb("uo_f", [2, N])
        pairs = sb("pairs", [2, C * CC])
        o_g = sb("o_g", [N])
        y_out = sb("y_out", [2, D])

        l_kfw = sb("l_kfw", [HD, 3, TB])
        l_q = sb("l_q", [HD, TB])
        l_u0 = sb("l_u0", [HD // 2, TB])
        prod = sb("prod", [TB, HD // 2, HD + 1])
        u_l = sb("u_l", [HD // 2, TB])
        outer = sb("outer", [2, HD, HD // 2, C + 1])
        state = sb("state", [NC + 1, HD, HD // 2])
        oprod = sb("oprod", [TB, HD // 2, HD])
        uo_l = sb("uo_l", [HD // 2, 2, TB])

        bank = [ctx.enter_context(nc.psum_tensor(f"bank{i}", [P, 512], F32)) for i in range(8)]
        left, right = (lambda i: bank[i][:, 0:N]), (lambda i: bank[i][:, N:2 * N])
        p_hid = [(left, right)[m % 2](m // 2) for m in range(4)]
        p_acc = left(2)
        p_cen, p_var, p_scale = left(3), bank[3][:, 0:2], left(3)
        p_qk0, p_k, p_q = bank[4][:, 0:QSPLIT * CC], left(4), right(4)
        p_g, p_fo, p_a = left(5), bank[5][0:2 * HD, N:2 * N], bank[5][:, 0:NPAIR * CC]
        p_out, p_z2, p_v, p_n, p_kscale = left(6), left(6), left(6), bank[6][:, 0:2 * H], left(6)
        p_qk1 = bank[5][:, 0:(NQPAIR - QSPLIT) * CC]
        p_wo, p_x, p_f, p_og, p_z1 = left(7), left(7), left(7), right(7), left(7)

        S = {}
        for name in ("w_first", "w_ffn", "w_attn", "x_in", "feat_stored", "kfw_head", "kfw_tail", "u0_head", "u0_tail",
                     "q_head", "q_tail", "uo_back", "y_stored",
                     "consts_pool", "consts_dve", "consts_fold", "w2_half", "setup", "setup_p", "fo_zero",
                     "xT_ps", "xT_sb", "z_ps1", "z_ps2", "m1_1", "m1_2", "m0_1", "m0_2",
                     "up1", "up2", "relu1", "relu2", "down1", "down2", "acc1", "acc2",
                     "y1", "y2", "y3",
                     "cenA", "cenB", "cenC", "cenD", "sqA", "sqB", "sqC", "sqD",
                     "varA", "varB", "varC", "varD", "csA", "csB", "csC", "csD",
                     "sdA", "sdB", "sdC", "sdD", "rsA", "rsB", "rsC", "rsD", "bcA", "bcB", "bcC", "bcD", "eps",
                     "nA", "nB", "nC", "nD",
                     "k_ps", "g_ps", "q_ps", "fo_ps", "v_ps", "f_ps", "og_ps",
                     "sig_k", "sig_g", "sig_q", "fo_sb", "v_sb", "f_sb", "fc0", "og_sb",
                     "k_raw", "q_sb", "k_sq", "n_ps", "k_floor", "k_len", "k_inv", "k_wide", "k_scale", "kn", "ag", "a_sb", "fc", "wt", "qt",
                     "rr", "ap", "qp", "a_ps", "fs_mul", "fs_add",
                     "u0_lane", "s0", "carried", "c_prod", "c_decay", "c_u", "c_outer", "c_state",
                     "oprod", "o_lane", "u_lane", "qk_ps", "mix_mul", "mix_add", "o_g", "wo_ps", "out_ps", "y_out"):
            S[name] = sem(name)

        def some(count):
            return not isinstance(count, int) or count > 0

        block = ctx.enter_context(nc.Block())

        def parts(n):
            return n < NB, 1 <= n <= NB, 2 <= n < NB + 2, ZL <= n < NB + ZL, n >= ZL + 1, n + 1 < NB

        STEADY = (ZL + 1, NB - 1)
        LAST = NB + ZL

        def run(eng, body):
            for n in range(STEADY[0]):
                body(n, *parts(n))
            with eng.Fori(STEADY[0], STEADY[1]) as n:
                body(n, *[True] * 6)
            for n in range(STEADY[1], LAST + 1):
                body(n, *parts(n))

        PV = (6, 9, 11, 13, 16, 19, 22)
        QV = (3, 5, 8, 10, 12, 13, 15, 17, 18, 20, 22)
        DP = (42, 46, 49, 51, 60, 64, 70, 73)
        DQ = (3, 6, 11, 15, 18, 22, 25)
        ORDER = (2, 1, 0)

        def at_most(n, top):
            return min(n, top) if isinstance(n, int) else n

        SLOTS = [("up", 0), ("up", 1)]
        for m in range(0, NM, 2):
            SLOTS += [("up", m + 2), ("up", m + 3)] if m + 2 < NM else []
            SLOTS += [("down", m), ("down", m + 1)]

        def ups(slots):
            return sum(kind == "up" for kind, _ in SLOTS[:slots]) // 2 * 2

        def steps(t, cc=CC):
            return t.rearrange("p (c j) -> p j c", j=C)

        featf = feat[:, :, :].rearrange("p a n -> p (a n)")
        key_diag = featf[:, 0:C * (N + 1)].rearrange("p (j r) -> p j r", r=N + 1)[:, :, 0:N - C + 1:C]
        keys = feat[:, 0:C, :].rearrange("p j (c s) -> p j c s", s=C)
        uw = feat[:, WW:U0 + 1:U0 - WW, :].rearrange("p x (c j) -> p x c j", j=C)

        @block.sync
        def _(sp):
            def load_x(n):
                for half in range(2):
                    src = x[2 * half:2 * half + 2, bass.ds(n * TB, TB), :]
                    sp.dma_start(x_in[:, half, :], src).then_inc(S["x_in"], 16)

            load_x(0)
            sp.dma_start(gate_sb[:, :], gate_w.rearrange("e d -> d e"), allow_slow_non_contiguous=True).then_inc(S["w_first"], 16)
            sp.dma_start(w1_sb[:, 0:2, :], w1.rearrange("e d h -> d e h")).then_inc(S["w_ffn"], 16)
            sp.dma_start(w1_sb[:, 2, :], sw1).then_inc(S["w_ffn"], 16)
            sp.dma_start(b1_sb[:, 0:2 * HC], b1.rearrange("e (c p) -> p (e c)", p=P), allow_slow_non_contiguous=True).then_inc(S["w_ffn"], 16)
            sp.dma_start(b1_sb[:, 2 * HC:NM], sb1.rearrange("(c p) -> p c", p=P), allow_slow_non_contiguous=True).then_inc(S["w_ffn"], 16)
            sp.dma_start(w2_sb[:, 0:2 * HC, :], w2.rearrange("e (c p) d -> p (e c) d", p=P)).then_inc(S["w_ffn"], 16)
            sp.dma_start(w2_sb[:, 2 * HC:NM, :], sw2.rearrange("(c p) d -> p c d", p=P)).then_inc(S["w_ffn"], 16)
            sp.dma_start(b2_sb[:, 0:2], b2.rearrange("e d -> d e"), allow_slow_non_contiguous=True).then_inc(S["w_ffn"], 16)
            sp.dma_start(b2_sb[:, 2:3], sb2.rearrange("(d a) -> d a", a=1), allow_slow_non_contiguous=True).then_inc(S["w_ffn"], 16)
            for dst, src in ((wq_sb, Wq), (wk_sb, Wk), (wv_sb, Wv), (wo_sb, Wo), (wgam_sb, Wgamma)):
                sp.dma_start(dst[:, :], src).then_inc(S["w_attn"], 16)
            sp.dma_start(wfo_sb[:, 0:HD], Wf1).then_inc(S["w_attn"], 16)
            sp.dma_start(wfo_sb[:, HD:2 * HD], Wog1).then_inc(S["w_attn"], 16)
            sp.wait_ge(S["fo_zero"], 2)
            sp.dma_start(wf2_sb[0:HD, :], Wf2).then_inc(S["w_attn"], 16)
            sp.dma_start(wog2_sb[HD:2 * HD, :], Wog2).then_inc(S["w_attn"], 16)
            sp.dma_start(nw_sb[:, :], norm_w.rearrange("(d a) -> d a", a=1), allow_slow_non_contiguous=True).then_inc(S["w_attn"], 16)

            def load_lanes(b, lo, hi, part):
                at, end = lo * C, hi * C
                before = NC * (b - 1) + hi
                if some(before):
                    sp.wait_ge(S["c_state"], before)
                for vh in range(2):
                    for a in range(3):
                        sp.dma_start(l_kfw[64 * vh:64 * vh + 64, :, a, at:end],
                                     kfw_dram[b][:, a, :, at:end].rearrange("(h k) b t -> b h k t", k=HD))\
                          .then_inc(S[("kfw_head", "kfw_tail")[part]], 16)
                if some(2 * b - 1 + part):
                    sp.wait_ge(S["u0_lane"], 2 * b - 1 + part)
                for vh in range(2):
                    sp.dma_start(l_u0[64 * vh:64 * vh + 64, :, at:end],
                                 qu_dram[b][:, 1, :, at:end].rearrange("(h v g) b t -> g b h v t", v=HD // 2, g=2)[vh])\
                      .then_inc(S[("u0_head", "u0_tail")[part]], 16)
                if some(before):
                    sp.wait_ge(S["oprod"], before)
                for vh in range(2):
                    sp.dma_start(l_q[64 * vh:64 * vh + 64, :, at:end],
                                 qu_dram[b][:, 0, :, at:end].rearrange("(h k) b t -> b h k t", k=HD))\
                      .then_inc(S[("q_head", "q_tail")[part]], 16)

            def body(n, first, head, tail, second, store, more):
                c, d, t = n - 1, n - 2, n - ZL - 1
                if more:
                    sp.wait_ge(S["xT_ps"], n + 1)
                    load_x(n + 1)
                if head:
                    sp.wait_ge(S["feat_stored"], 32 * (c + 1))
                    load_lanes(c, 0, SPLIT, 0)
                if store:
                    sp.wait_ge(S["y_out"], t + 1)
                    for half in range(2):
                        sp.dma_start(out[2 * half:2 * half + 2, bass.ds(t * TB, TB), :],
                                     y_out[:, half, :]).then_inc(S["y_stored"], 16)
                if tail:
                    sp.wait_ge(S["u_lane"], d + 1)
                    sp.wait_ge(S["o_lane"], 2 * (d + 1))
                    if some(d):
                        sp.wait_ge(S["mix_add"], C * d)
                        sp.wait_ge(S["o_g"], d)
                    for vh in range(2):
                        for b in range(B):
                            sp.dma_start(uo_f[vh:P:2, :, TB * b:TB * b + TB],
                                         uo_l[64 * vh + H * b:64 * vh + H * b + H, :, :, :]).then_inc(S["uo_back"], 16)
                if head:
                    load_lanes(c, SPLIT, NC, 1)
                if first:
                    sp.wait_ge(S["fs_add"], 3 * (n + 1))
                    sp.wait_ge(S["qt"], n + 1)
                    sp.wait_ge(S["rr"], 3 * (n + 1))
                    sp.dma_start(kfw_dram[n].rearrange("p a b t -> p (a b t)"),
                                 feat[:, KH:WW + 1, :]).then_inc(S["feat_stored"], 16)
                    sp.dma_start(qu_dram[n].rearrange("p a b t -> p (a b t)"),
                                 feat[:, QT:U0 + 1, :]).then_inc(S["feat_stored"], 16)
            for n in range(LAST + 1):
                body(n, *parts(n))
            sp.wait_ge(S["y_stored"], 32 * NB + 1)

        @block.tensor
        def _(pe):
            mm = nc.tensor.matmul

            def slot(tag, b, i):
                kind, m = SLOTS[i]
                e, w = ORDER[m // HC], ORDER[m // HC] * HC + m % HC
                if kind == "up":
                    if m == 0:
                        pe.wait_ge(S[("nA", "nD")[tag - 1]], b + 1)
                    if m == HC:
                        pe.wait_ge(S[f"m1_{tag}"], b + 1)
                    if m == 2 * HC:
                        pe.wait_ge(S[f"m0_{tag}"], b + 1)
                    if m in (0, 2):
                        other = (b - ZL, at_most(b + ZL + 1, NB))[tag - 1]
                        if some(NM * other - 2 + m):
                            pe.wait_ge(S[f"relu{3 - tag}"], NM * other - 2 + m)
                    if m % 2 == 0:
                        if some(NM * b + m - 2):
                            pe.wait_ge(S[f"relu{tag}"], NM * b + m - 2)
                    src = {2: (xn1, xn2), 1: (m1_1, m1_2), 0: (m0_1, m0_2)}[e][tag - 1]
                    mm(p_hid[m % 4], w1_sb[:, e, P * (m % HC):P * (m % HC) + P], src[:, :],
                       start=True, stop=True).then_inc(S[f"up{tag}"], 1)
                else:
                    if m == 0:
                        if some(b):
                            pe.wait_ge(S[("y1", "y3")[tag - 1]], b)
                        if some((b - ZL, at_most(b + ZL + 1, NB))[tag - 1]):
                            pe.wait_ge(S[("y3", "y1")[tag - 1]], (b - ZL, at_most(b + ZL + 1, NB))[tag - 1])
                    pe.wait_ge(S[f"relu{tag}"], NM * b + m + 1)
                    mm(p_acc, w2_sb[:, w, :], hid[:, m % 4, :], start=m == 0, stop=m == NM - 1)\
                        .then_inc(S[f"down{tag}"], 1)

            def ffn(tag, b, lo, hi, there):
                if there:
                    for i in range(lo, hi):
                        slot(tag, b, i)

            def transposed_in(b):
                pe.wait_ge(S["x_in"], 32 * (b + 1))
                if some(b):
                    pe.wait_ge(S["m1_1"], b)
                for half in range(2):
                    last = nc.tensor.transpose(p_x[:, P * half:P * half + P], x_in[:, half, :], ident[:, :])
                last.then_inc(S["xT_ps"], 1)

            def centered(tag, b, src, ready):
                pe.wait_ge(S[ready], b + 1)
                mm(p_cen, center[:, :], src, start=True, stop=True).then_inc(S["cen" + tag], 1)

            def variance(tag, b):
                pe.wait_ge(S["sq" + tag], b + 1)
                pe.wait_ge(S["cs" + tag], b + 1)
                for half in range(2):
                    last = mm(p_var[:, half:half + 1], sq[:, P * half:P * half + P], average[:, 0:1], start=True, stop=True)
                last.then_inc(S["var" + tag], 1)

            def spread(tag, b):
                pe.wait_ge(S["rs" + tag], b + 1)
                for half in range(2):
                    last = mm(p_scale[:, P * half:P * half + P], rsd[:, half:half + 1].to_broadcast([P, P]), ident[:, :],
                              start=True, stop=True)
                last.then_inc(S["bc" + tag], 1)

            def routed(tag, b, src):
                pe.wait_ge(S[("nA", "nD")[tag - 1]], b + 1)
                mm((p_z1, p_z2)[tag - 1], gate_bc[:, :], src[:, :], start=True, stop=True).then_inc(S[f"z_ps{tag}"], 1)

            pe.wait_ge(S["setup_p"], 3)
            pe.wait_ge(S["setup"], 5)
            pe.wait_ge(S["w_ffn"], 16 * 8)
            pe.wait_ge(S["w_attn"], 16 * 10)
            transposed_in(0)
            centered("A", 0, xT[:, :], "xT_sb")
            variance("A", 0)
            spread("A", 0)
            routed(1, 0, xn1)

            def body(n, first, head, tail, second, store, more):
                d, z, t = n - 2, n - ZL, n - ZL - 1
                ffn(1, n, 0, 2, first)
                if second:
                    pe.wait_ge(S["nA"], at_most(n + 1, NB))
                    if some(z):
                        pe.wait_ge(S["nD"], z)
                    centered("C", z, o_g[:, :], "o_g")
                ffn(1, n, 2, 4, first)
                if store:
                    pe.wait_ge(S["y3"], t + 1)
                    if some(at_most(n, NB)):
                        pe.wait_ge(S["kn"], at_most(n, NB))
                    pe.wait_ge(S["m1_2"], z)
                    for half in range(2):
                        last = nc.tensor.transpose(p_out[:, P * half:P * half + P], y3T[:, P * half:P * half + P], ident[:, :])
                    last.then_inc(S["out_ps"], 1)
                ffn(1, n, 4, PV[0], first)
                if second:
                    variance("C", z)
                ffn(1, n, PV[0], PV[1], first)
                if second:
                    spread("C", z)
                ffn(1, n, PV[1], PV[2], first)
                if second:
                    pe.wait_ge(S["nC"], z + 1)
                    pe.wait_ge(S["m1_1"], at_most(n + 1, NB))
                    if some(z):
                        pe.wait_ge(S["y2"], z)
                    mm(p_wo, wo_sb[:, :], onT[:, :], start=True, stop=True).then_inc(S["wo_ps"], 1)
                ffn(1, n, PV[2], PV[3], first)
                if second:
                    centered("D", z, y2T[:, :], "y2")
                ffn(1, n, PV[3], PV[4], first)
                if second:
                    variance("D", z)
                ffn(1, n, PV[4], PV[5], first)
                if second:
                    spread("D", z)
                ffn(1, n, PV[5], PV[6], first)
                if second:
                    if some(z):
                        pe.wait_ge(S["y_out"], z)
                    pe.wait_ge(S["kn"], at_most(n, NB))
                    routed(2, z, xn2)
                ffn(1, n, PV[6], 24, first)

                ffn(2, z, 0, QV[0], second)
                if first:
                    pe.wait_ge(S["nA"], n + 1)
                    if second:
                        pe.wait_ge(S["nD"], z + 1)
                    centered("B", n, y1T[:, n, :], "y1")
                if more:
                    if second:
                        pe.wait_ge(S["y2"], z + 1)
                    transposed_in(n + 1)
                ffn(2, z, QV[0], QV[1], second)
                if first:
                    variance("B", n)
                ffn(2, z, QV[1], QV[2], second)
                if first:
                    spread("B", n)
                ffn(2, z, QV[2], QV[3], second)
                if first:
                    pe.wait_ge(S["nB"], n + 1)
                    if some(3 * n):
                        pe.wait_ge(S["fs_mul"], 3 * n)
                    if some(C * (n - 2)):
                        pe.wait_ge(S["mix_mul"], C * (n - 2))
                    mm(p_fo, wfo_sb[:, :], xnB[:, :], start=True, stop=True).then_inc(S["fo_ps"], 1)
                    mm(p_g, wgam_bc[:, :, :], xnB[:, :], start=True, stop=True).then_inc(S["g_ps"], 1)
                    if some(n):
                        pe.wait_ge(S["q_sb"], n)
                    mm(p_k, wk_sb[:, :], xnB[:, :], start=True, stop=True).then_inc(S["k_ps"], 1)
                    mm(p_q, wq_sb[:, :], xnB[:, :], start=True, stop=True).then_inc(S["q_ps"], 1)
                    if some(n):
                        pe.wait_ge(S["kn"], n)
                    if second:
                        pe.wait_ge(S["m1_2"], z + 1)
                    mm(p_v, wv_sb[:, :], xnB[:, :], start=True, stop=True).then_inc(S["v_ps"], 1)
                ffn(2, z, QV[3], QV[4], second)
                if first:
                    pe.wait_ge(S["fo_sb"], n + 1)
                    pe.wait_ge(S["m1_1"], n + 1)
                    if second:
                        pe.wait_ge(S["y2"], z + 1)
                    if more:
                        pe.wait_ge(S["xT_sb"], n + 2)
                    mm(p_f, wf2_sb[0:2 * HD, :], fo[0:2 * HD, :], start=True, stop=True).then_inc(S["f_ps"], 1)
                    mm(p_og, wog2_sb[0:2 * HD, :], fo[0:2 * HD, :], start=True, stop=True).then_inc(S["og_ps"], 1)
                ffn(2, z, QV[4], QV[5], second)
                if more:
                    pe.wait_ge(S["nB"], n + 1)
                    centered("A", n + 1, xT[:, :], "xT_sb")
                ffn(2, z, QV[5], QV[6], second)
                if first:
                    pe.wait_ge(S["k_sq"], n + 1)
                    pe.wait_ge(S["v_sb"], n + 1)
                    for half in range(2):
                        last = mm(p_n[:, H * half:H * half + H], k_sq[:, P * half:P * half + P], heads[:, 0:P:HD],
                                  start=True, stop=True)
                    last.then_inc(S["n_ps"], 1)
                ffn(2, z, QV[6], QV[7], second)
                if more:
                    variance("A", n + 1)
                if tail:
                    pe.wait_ge(S["qp"], C * (d + 1))
                    if some(C * d):
                        pe.wait_ge(S["mix_mul"], C * d)
                    if first:
                        pe.wait_ge(S["q_sb"], n + 1)
                        pe.wait_ge(S["fo_sb"], n + 1)
                        pe.wait_ge(S["sig_g"], n + 1)
                    mm(p_qk0, heads[:, :], qp[:, d, 0:QSPLIT, :], start=True, stop=True)
                    if some(3 * at_most(n, NB)):
                        pe.wait_ge(S["fs_mul"], 3 * at_most(n, NB))
                    mm(p_qk1, heads[:, :], qp[:, d, QSPLIT:NQPAIR, :], start=True, stop=True).then_inc(S["qk_ps"], 1)
                ffn(2, z, QV[7], QV[8], second)
                if first:
                    pe.wait_ge(S["k_wide"], n + 1)
                    for half in range(2):
                        last = mm(p_kscale[:, P * half:P * half + P],
                                  k_wide[:, half, :], ident[:, :], start=True, stop=True)
                    last.then_inc(S["k_scale"], 1)
                ffn(2, z, QV[8], QV[9], second)
                if more:
                    spread("A", n + 1)
                ffn(2, z, QV[9], QV[10], second)
                if more:
                    pe.wait_ge(S["og_sb"], n + 1)
                    routed(1, n + 1, xn1)
                ffn(2, z, QV[10], 24, second)
                if first:
                    pe.wait_ge(S["ap"], 3 * (n + 1))
                    if tail:
                        pe.wait_ge(S["mix_mul"], C * (d + 1))
                    pe.wait_ge(S["fo_sb"], n + 1)
                    pe.wait_ge(S["sig_g"], n + 1)
                    mm(p_a, heads[:, :], ap_[:, :, :], start=True, stop=True).then_inc(S["a_ps"], 1)
            run(pe, body)

        @block.scalar
        def _(act):
            def relu(tag, b, lo, hi, there):
                if there:
                    for m in range(ups(lo), ups(hi)):
                        w = ORDER[m // HC] * HC + m % HC
                        act.wait_ge(S[f"up{tag}"], NM * b + m // 2 * 2 + 2)
                        if m < 4:
                            other = (b - ZL, at_most(b + ZL + 1, NB))[tag - 1]
                            if some(NM * other - 3 + m):
                                act.wait_ge(S[f"down{3 - tag}"], NM * other - 3 + m)
                        if some(NM * b + m - 3):
                            act.wait_ge(S[f"down{tag}"], NM * b + m - 3)
                        nc.scalar.activation(hid[:, m % 4, :], p_hid[m % 4], ACT.Relu, bias=b1_sb[:, w:w + 1])\
                            .then_inc(S[f"relu{tag}"], 1)

            def centred(tag, b):
                act.wait_ge(S["cen" + tag], b + 1)
                nc.scalar.activation(sq[:, :], p_cen, ACT.Square).then_inc(S["sq" + tag], 1)
                nc.scalar.copy(cen[:, :], p_cen).then_inc(S["cs" + tag], 1)

            def deviation(tag, b):
                act.wait_ge(S["var" + tag], b + 1)
                nc.scalar.activation(sd[:, :], p_var, ACT.Sqrt, bias=eps[:, :]).then_inc(S["sd" + tag], 1)

            def x_copy(b):
                act.wait_ge(S["xT_ps"], b + 1)
                if some(b):
                    act.wait_ge(S["y1"], b)
                nc.scalar.copy(xT[:, :], p_x).then_inc(S["xT_sb"], 1)

            act.wait_ge(S["w_ffn"], 16 * 8)
            act.wait_ge(S["eps"], 1)
            x_copy(0)
            centred("A", 0)
            deviation("A", 0)

            def body(n, first, head, tail, second, store, more):
                z, t = n - ZL, n - ZL - 1
                relu(1, n, 0, 2, first)
                if second:
                    act.wait_ge(S["nA"], at_most(n + 1, NB))
                    if some(z):
                        act.wait_ge(S["nD"], z)
                    centred("C", z)
                relu(1, n, 2, 4, first)
                if store:
                    act.wait_ge(S["out_ps"], t + 1)
                    act.wait_ge(S["y_stored"], 32 * t + 1)
                    nc.scalar.copy(y_out[:, :, :], p_out.rearrange("p (h d) -> p h d", h=2)).then_inc(S["y_out"], 1)
                relu(1, n, 4, PV[0], first)
                if second:
                    deviation("C", z)
                relu(1, n, PV[0], PV[3], first)
                if second:
                    act.wait_ge(S["nC"], z + 1)
                    centred("D", z)
                relu(1, n, PV[3], PV[4], first)
                if second:
                    deviation("D", z)
                relu(1, n, PV[4], 24, first)

                relu(2, z, 0, QV[0], second)
                if first:
                    act.wait_ge(S["nA"], n + 1)
                    if second:
                        act.wait_ge(S["nD"], z + 1)
                    centred("B", n)
                if more:
                    x_copy(n + 1)
                relu(2, z, QV[0], QV[1], second)
                if first:
                    deviation("B", n)
                relu(2, z, QV[1], QV[3], second)
                if first:
                    act.wait_ge(S["g_ps"], n + 1)
                    nc.scalar.copy(fo[0:2 * HD, :], p_fo).then_inc(S["fo_sb"], 1)
                    act.wait_ge(S["q_ps"], n + 1)
                    if some(n):
                        act.wait_ge(S["k_raw"], n)
                    nc.scalar.activation(sig_k[:, :], p_k, ACT.Sigmoid).then_inc(S["sig_k"], 1)
                    if some(n):
                        act.wait_ge(S["q_sb"], n)
                    nc.scalar.activation(sig_q[:, :], p_q, ACT.Sigmoid).then_inc(S["sig_q"], 1)
                    if some(n):
                        act.wait_ge(S["ag"], n)
                    nc.scalar.activation(sig_g[:, :], p_g, ACT.Sigmoid).then_inc(S["sig_g"], 1)
                    act.wait_ge(S["v_ps"], n + 1)
                    if some(32 * n):
                        act.wait_ge(S["feat_stored"], 32 * n)
                    nc.scalar.copy(feat[:, U0, :], p_v).then_inc(S["v_sb"], 1)
                relu(2, z, QV[3], QV[4], second)
                if first:
                    act.wait_ge(S["og_ps"], n + 1)
                    if some(3 * n):
                        act.wait_ge(S["rr"], 3 * n)
                    if some(n):
                        act.wait_ge(S["a_sb"], n)
                    nc.scalar.activation(f[:, :], p_f, ACT.Sigmoid).then_inc(S["f_sb"], 1)
                    nc.scalar.activation(steps(feat[:, FC, :])[:, 0], steps(p_f)[:, 0], ACT.Sigmoid).then_inc(S["fc0"], 1)
                    act.wait_ge(S["k_raw"], n + 1)
                    nc.scalar.activation(k_sq[:, :], k_raw[:, :], ACT.Square).then_inc(S["k_sq"], 1)
                    nc.scalar.activation(og[:, n, :], p_og, ACT.Sigmoid).then_inc(S["og_sb"], 1)
                relu(2, z, QV[4], QV[5], second)
                if more:
                    act.wait_ge(S["nB"], n + 1)
                    centred("A", n + 1)
                relu(2, z, QV[5], QV[6], second)
                if first:
                    act.wait_ge(S["k_floor"], n + 1)
                    nc.scalar.activation(k_len[:, :, :], k_floor[:, :, :], ACT.Sqrt).then_inc(S["k_len"], 1)
                relu(2, z, QV[6], QV[7], second)
                if first:
                    act.wait_ge(S["k_inv"], n + 1)
                    nc.scalar.copy(k_wide[:, :, :].rearrange("p a (h k) -> p a h k", k=HD),
                                   k_inv[:, :, :, None].to_broadcast([P, 2, H, HD])).then_inc(S["k_wide"], 1)
                if more:
                    deviation("A", n + 1)
                relu(2, z, QV[7], 24, second)
            run(act, body)

        @block.vector
        def _(dve):
            tt, ts, stt = nc.vector.tensor_tensor, nc.vector.tensor_scalar, nc.vector.scalar_tensor_tensor

            nc.vector.memset(wf2_sb[0:2 * HD, :], 0.0).then_inc(S["fo_zero"], 1)
            nc.vector.memset(wog2_sb[0:2 * HD, :], 0.0).then_inc(S["fo_zero"], 1)
            nc.vector.memset(eps[:, :], EPS).then_inc(S["eps"], 1)
            nc.vector.memset(y_out[:, :, :], 0.0).then_inc(S["y_stored"], 1)
            nc.vector.memset(state[:, NC, :, :], 0.0).then_inc(S["s0"], 1)
            dve.wait_ge(S["w_first"], 16)
            tt(gate_diff[:, :], gate_sb[:, 1:2], gate_sb[:, 0:1], ALU.subtract).then_inc(S["consts_dve"], 1)
            dve.wait_ge(S["consts_dve"], 1)
            dve.wait_ge(S["consts_pool"], 2)
            ts(gate_bc[:, :], average[:, :], 0.0, gate_diff[:, :], ALU.mult, ALU.add).then_inc(S["setup"], 1)
            dve.wait_ge(S["w_ffn"], 16 * 8)
            nc.vector.tensor_reduce(hb2[:, :], b2_sb[:, :], axis=AX.X, op=ALU.add).then_inc(S["consts_dve"], 1)
            ts(w2_sb[:, :, :], w2_sb[:, :, :], 0.5, None, ALU.mult).then_inc(S["setup"], 1)
            dve.wait_ge(S["consts_dve"], 2)
            ts(hb2[:, :], hb2[:, :], 0.5, None, ALU.mult).then_inc(S["setup"], 1)
            dve.wait_ge(S["w_attn"], 16 * 10)
            ts(wo_sb[:, :], wo_sb[:, :], nw_sb[:, :], None, ALU.mult).then_inc(S["setup"], 1)
            nc.vector.tensor_copy(wgam_bc[:, :, :], wgam_sb[:, :, None].to_broadcast([P, H, HD])).then_inc(S["setup"], 1)
            dve.wait_ge(S["setup"], 5)

            def inverse_deviation(tag, b):
                dve.wait_ge(S["sd" + tag], b + 1)
                nc.vector.reciprocal(rsd[:, :], sd[:, :]).then_inc(S["rs" + tag], 1)

            def normalised(tag, b, dst):
                dve.wait_ge(S["bc" + tag], b + 1)
                dve.wait_ge(S["cs" + tag], b + 1)
                tt(dst[:, :], cen[:, :], p_scale, ALU.mult).then_inc(S["n" + tag], 1)

            def routing(tag, b, src, dst):
                dve.wait_ge(S[f"z_ps{tag}"], b + 1)
                stt(dst[:, :], (p_z1, p_z2)[tag - 1], 0.0, src[:, :], ALU.is_gt, ALU.mult).then_inc(S[f"m1_{tag}"], 1)

            inverse_deviation("A", 0)
            normalised("A", 0, xn1)
            routing(1, 0, xn1, m1_1)

            def scan_op(b, i):
                c, kind = divmod(i, 5)
                done = NC * b + c
                steps_c = slice(C * c, C * c + C)
                now, nxt = c, c + 1
                if kind == 0:
                    if c in (0, SPLIT):
                        part, part_end = ((0, SPLIT), (1, NC))[c > 0]
                        part_steps = slice(C * c, C * part_end)
                        dve.wait_ge(S[("u0_head", "u0_tail")[part]], 32 * (b + 1))
                        if some(NC * (b - 1) + part_end):
                            dve.wait_ge(S["c_u"], NC * (b - 1) + part_end)
                        nc.vector.tensor_copy(prod[:, part_steps, :, HD], l_u0[:, :, part_steps].rearrange("p v t -> p t v"))\
                            .then_inc(S["u0_lane"], 1)
                        if some(NC * (b - 1) + part_end):
                            dve.wait_ge(S["oprod"], NC * (b - 1) + part_end)
                        if c == 0:
                            if some(b):
                                dve.wait_ge(S["oprod"], NC * (b - 1) + SPLIT + 1)
                                dve.wait_ge(S["c_state"], NC * b)
                            dve.wait_ge(S["s0"], 1)
                            nc.vector.tensor_copy(state[:, 0], state[:, NC]).then_inc(S["carried"], 1)
                            dve.wait_ge(S["carried"], b + 1)
                        dve.wait_ge(S[("kfw_head", "kfw_tail")[part]], 96 * (b + 1))
                    if some(done):
                        dve.wait_ge(S["c_state"], done)
                    tt(prod[:, steps_c, :, 0:HD],
                       l_kfw[:, :, 2, steps_c].rearrange("p k j -> p j k")[:, :, None, :].to_broadcast([P, C, HD // 2, HD]),
                       state[:, now].rearrange("p k v -> p v k")[:, None].to_broadcast([P, C, HD // 2, HD]),
                       ALU.mult).then_inc(S["c_prod"], 1)
                elif kind == 1:
                    tt(outer[:, c % 2, :, :, C],
                       l_kfw[:, :, 1, C * c + C - 1][:, :, None].to_broadcast([P, HD, HD // 2]),
                       state[:, now], ALU.mult).then_inc(S["c_decay"], 1)
                elif kind == 2:
                    if c in (0, SPLIT):
                        dve.wait_ge(S["u0_lane"], 2 * b + 1 + (c > 0))
                    if c == 0:
                        if some(b):
                            dve.wait_ge(S["u_lane"], b)
                    dve.wait_ge(S["c_prod"], done + 1)
                    nc.vector.tensor_reduce(u_l[:, :, steps_c].rearrange("p v j -> p j v"), prod[:, steps_c],
                                            axis=AX.X, op=ALU.add).then_inc(S["c_u"], 1)
                elif kind == 3:
                    dve.wait_ge(S["c_u"], done + 1)
                    tt(outer[:, c % 2, :, :, 0:C],
                       l_kfw[:, :, 0, steps_c][:, :, None, :].to_broadcast([P, HD, HD // 2, C]),
                       u_l[:, :, steps_c][:, None].to_broadcast([P, HD, HD // 2, C]),
                       ALU.mult).then_inc(S["c_outer"], 1)
                else:
                    dve.wait_ge(S["c_decay"], done + 1)
                    dve.wait_ge(S["c_outer"], done + 1)
                    nc.vector.tensor_reduce(state[:, nxt], outer[:, c % 2], axis=AX.X, op=ALU.add)\
                        .then_inc(S["c_state"], 1)

            def scan(b, lo, hi, there):
                if there:
                    for i in range(lo, hi):
                        scan_op(b, i)

            def state_output(b, half):
                rows = slice(TB // 2 * half, TB // 2 * (half + 1))
                if some(16 * 8 * b):
                    dve.wait_ge(S["uo_back"], 16 * 8 * b)
                dve.wait_ge(S["oprod"], NC * b + NC // 2 * (half + 1))
                nc.vector.tensor_reduce(uo_l[:, :, 1, rows].rearrange("p v t -> p t v"), oprod[:, rows, :, :],
                                        axis=AX.X, op=ALU.add).then_inc(S["o_lane"], 1)

            def mix(b, s):
                if s == 0:
                    dve.wait_ge(S["qk_ps"], b + 1)
                    dve.wait_ge(S["uo_back"], 16 * 8 * (b + 1))
                width = (C - s) * CC
                pair = (p_qk0 if s < 2 else p_qk1)
                at = (QPAIRS[s] - (0 if s < 2 else QSPLIT)) * CC
                if some(C * b + s - 1):
                    dve.wait_ge(S["mix_add"], C * b + s - 1)
                tt(pairs[:, s % 2, 0:width].rearrange("p (j c) -> p j c", c=CC),
                   pair[:, at:at + width].rearrange("p (j c) -> p j c", c=CC),
                   steps(uo_f[:, 0, :])[:, s][:, None].to_broadcast([P, C - s, CC]), ALU.mult).then_inc(S["mix_mul"], 1)

            def mixed(b, s):
                width = (C - s) * CC
                dve.wait_ge(S["mix_mul"], C * b + s + 1)
                if some(C * b + s):
                    dve.wait_ge(S["mix_add"], C * b + s)
                tt(steps(uo_f[:, 1, :])[:, s:C], pairs[:, s % 2, 0:width].rearrange("p (j c) -> p j c", c=CC),
                   steps(uo_f[:, 1, :])[:, s:C], ALU.add).then_inc(S["mix_add"], 1)

            def body(n, first, head, tail, second, store, more):
                c, d, z = n - 1, n - 2, n - ZL
                scan(d, 5 * SPLIT, DP[0], tail)
                if second:
                    inverse_deviation("C", z)
                scan(d, DP[0], DP[1], tail)
                if second:
                    normalised("C", z, onT)
                scan(d, DP[1], DP[2], tail)
                if second:
                    dve.wait_ge(S["wo_ps"], z + 1)
                    tt(y2T[:, :], p_wo, y1T[:, z, :], ALU.add).then_inc(S["y2"], 1)
                scan(d, DP[2], DP[3], tail)
                if tail:
                    state_output(d, 0)
                scan(d, DP[3], DP[4], tail)
                if second:
                    inverse_deviation("D", z)
                scan(d, DP[4], DP[5], tail)
                if second:
                    normalised("D", z, xn2)
                scan(d, DP[5], DP[6], tail)
                if second:
                    routing(2, z, xn2, m1_2)
                scan(d, DP[6], DP[7], tail)
                if first:
                    dve.wait_ge(S["down1"], NM * (n + 1))
                    stt(y1T[:, n, :], p_acc, hb2[:, :], xT[:, :], ALU.add, ALU.add).then_inc(S["y1"], 1)
                scan(d, DP[7], 80, tail)
                if tail:
                    dve.wait_ge(S["c_u"], NC * (d + 1))
                    if some(16 * 8 * d):
                        dve.wait_ge(S["uo_back"], 16 * 8 * d)
                    nc.vector.tensor_copy(uo_l[:, :, 0, :], u_l[:, :, :]).then_inc(S["u_lane"], 1)
                    state_output(d, 1)

                if first:
                    inverse_deviation("B", n)
                scan(c, 0, DQ[0], head)
                if first:
                    normalised("B", n, xnB)
                scan(c, DQ[0], DQ[1], head)
                if first:
                    dve.wait_ge(S["sig_q"], n + 1)
                    tt(k_raw[:, :], p_k, sig_k[:, :], ALU.mult).then_inc(S["k_raw"], 1)
                    if some(n):
                        dve.wait_ge(S["qt"], n)
                        dve.wait_ge(S["qp"], C * n)
                    tt(q[:, :], p_q, sig_q[:, :], ALU.mult).then_inc(S["q_sb"], 1)
                scan(c, DQ[1], DQ[2], head)
                if first:
                    dve.wait_ge(S["n_ps"], n + 1)
                    ts(k_floor[:, :, :], p_n.rearrange("p (a h) -> p a h", a=2), 1e-24, None, ALU.max).then_inc(S["k_floor"], 1)
                scan(c, DQ[2], DQ[3], head)
                if first:
                    dve.wait_ge(S["k_len"], n + 1)
                    nc.vector.reciprocal(k_inv[:, :, :], k_len[:, :, :]).then_inc(S["k_inv"], 1)
                if more:
                    inverse_deviation("A", n + 1)
                if tail:
                    mix(d, 0)
                    mix(d, 1)
                    mixed(d, 0)
                if first:
                    dve.wait_ge(S["k_scale"], n + 1)
                    if some(n):
                        dve.wait_ge(S["qp"], C * n)
                        dve.wait_ge(S["feat_stored"], 32 * n)
                    tt(key_diag, steps(k_raw[:, :]), steps(p_kscale), ALU.mult).then_inc(S["kn"], 1)
                if tail:
                    mixed(d, 1)
                    mix(d, 2)
                    mix(d, 3)
                if more:
                    normalised("A", n + 1, xn1)
                if first:
                    dve.wait_ge(S["kn"], n + 1)
                    dve.wait_ge(S["sig_g"], n + 1)
                    if some(n):
                        dve.wait_ge(S["a_sb"], n)
                    stt(steps(ag[:, :]), key_diag, -1.0, steps(sig_g[:, :]), ALU.mult, ALU.mult).then_inc(S["ag"], 1)
                if tail:
                    mixed(d, 2)
                scan(c, DQ[3], DQ[4], head)
                if tail:
                    mixed(d, 3)
                if more:
                    routing(1, n + 1, xn1, m1_1)
                scan(c, DQ[4], DQ[5], head)
                if first:
                    dve.wait_ge(S["rr"], 3 * (n + 1))
                    dve.wait_ge(S["a_sb"], n + 1)
                    for s in range(C - 1):
                        tt(ap_[:, PAIRS[s]:PAIRS[s] + C - 1 - s, :], steps(a[:, :])[:, s + 1:C], keys[:, s + 1:C, :, s],
                           ALU.mult).then_inc(S["ap"], 1)
                scan(c, DQ[5], DQ[6], head)
                if second:
                    dve.wait_ge(S["down2"], NM * (z + 1))
                    if some(z):
                        dve.wait_ge(S["out_ps"], z)
                    stt(y3T[:, :], p_acc, hb2[:, :], y2T[:, :], ALU.add, ALU.add).then_inc(S["y3"], 1)
                if first:
                    dve.wait_ge(S["a_ps"], n + 1)
                    dve.wait_ge(S["wt"], n + 1)
                    dve.wait_ge(S["v_sb"], n + 1)
                    for s in range(C - 1):
                        left = C - 1 - s
                        tmp = solve[:, 0:left * 2 * CC].rearrange("p (j x c) -> p j x c", x=2, c=CC)
                        if some(3 * n + s):
                            dve.wait_ge(S["fs_add"], 3 * n + s)
                        tt(tmp, p_a.rearrange("p (j c) -> p j c", c=CC)[:, PAIRS[s]:PAIRS[s] + left][:, :, None]
                           .to_broadcast([P, left, 2, CC]),
                           uw[:, :, :, s][:, None].to_broadcast([P, left, 2, CC]), ALU.mult).then_inc(S["fs_mul"], 1)
                        scan(c, DQ[6] + 2 * s, DQ[6] + 1 + 2 * s, head)
                        dve.wait_ge(S["fs_mul"], 3 * n + s + 1)
                        dst = uw[:, :, :, s + 1:C].rearrange("p x c j -> p j x c")
                        tt(dst, tmp, dst, ALU.add).then_inc(S["fs_add"], 1)
                        scan(c, DQ[6] + 1 + 2 * s, DQ[6] + 2 + 2 * s, head)
                    scan(c, DQ[6] + 6, 5 * SPLIT, head)
                else:
                    scan(c, DQ[6], 5 * SPLIT, head)
            run(dve, body)

        @block.gpsimd
        def _(pool):
            tt = nc.gpsimd.tensor_tensor
            nc.gpsimd.memset(ident[:, :], 0.0).then_inc(S["consts_pool"], 1)
            nc.gpsimd.memset(average[:, :], 1.0 / D).then_inc(S["consts_pool"], 1)
            nc.gpsimd.memset(heads[:, :], 1.0).then_inc(S["consts_pool"], 1)
            pool.wait_ge(S["consts_pool"], 3)
            nc.gpsimd.affine_select(out=ident[:, :], in_=ident[:, :], compare_op=ALU.not_equal, fill=1.0, base=0,
                                    pattern=[[-1, P]], channel_multiplier=1).then_inc(S["setup_p"], 1)
            hv = heads[:, :].rearrange("p (h k) -> p h k", k=HD)
            nc.gpsimd.affine_select(out=hv, in_=hv, compare_op=ALU.is_ge, fill=0.0, base=0,
                                    pattern=[[-HD, H], [0, HD]], channel_multiplier=1).then_inc(S["consts_fold"], 1)
            pool.wait_ge(S["consts_fold"], 1)
            nc.gpsimd.affine_select(out=hv, in_=hv, compare_op=ALU.is_ge, fill=0.0, base=HD - 1,
                                    pattern=[[HD, H], [0, HD]], channel_multiplier=-1).then_inc(S["setup_p"], 1)
            pool.wait_ge(S["setup_p"], 2)
            tt(center[:, :], ident[:, :], average[:, :], ALU.subtract).then_inc(S["setup_p"], 1)

            def rest(tag, b, whole, one, dst):
                pool.wait_ge(S[f"m1_{tag}"], b + 1)
                tt(dst[:, :], whole[:, :], one[:, :], ALU.subtract).then_inc(S[f"m0_{tag}"], 1)

            rest(1, 0, xn1, m1_1, m0_1)

            def state_products(b, lo, hi, there):
                for i in range(lo, hi) if there else ():
                    if i == 0:
                        pool.wait_ge(S["carried"], b + 1)
                        if some(2 * b - 1):
                            pool.wait_ge(S["o_lane"], 2 * b - 1)
                    else:
                        pool.wait_ge(S["c_state"], NC * b + i)
                    if i == NC // 2 and some(2 * b):
                        pool.wait_ge(S["o_lane"], 2 * b)
                    if i in (0, SPLIT):
                        pool.wait_ge(S[("q_head", "q_tail")[i > 0]], 32 * (b + 1))
                    rows = slice(C * i, C * i + C)
                    tt(oprod[:, rows, :, :],
                       l_q[:, :, rows].rearrange("p k t -> p t k")[:, :, None, :].to_broadcast([P, C, HD // 2, HD]),
                       state[:, i].rearrange("p k v -> p v k")[:, None].to_broadcast([P, C, HD // 2, HD]),
                       ALU.mult).then_inc(S["oprod"], 1)

            def body(n, first, head, tail, second, store, more):
                c, d, z = n - 1, n - 2, n - ZL
                state_products(d, SPLIT, 12, tail)
                if second:
                    rest(2, z, xn2, m1_2, m0_2)
                state_products(d, 12, NC, tail)
                if first:
                    pool.wait_ge(S["f_sb"], n + 1)
                    pool.wait_ge(S["fc0"], n + 1)
                    for j in range(1, C):
                        if some(3 * n + j - 1):
                            pool.wait_ge(S["fc"], 3 * n + j - 1)
                        tt(steps(feat[:, FC, :])[:, j], steps(feat[:, FC, :])[:, j - 1], steps(f[:, :])[:, j], ALU.mult)\
                            .then_inc(S["fc"], 1)
                    pool.wait_ge(S["q_sb"], n + 1)
                    pool.wait_ge(S["fc"], 3 * (n + 1))
                    tt(feat[:, QT, :], q[:, :], feat[:, FC, :], ALU.mult).then_inc(S["qt"], 1)
                    pool.wait_ge(S["kn"], n + 1)
                    for j in range(1, C):
                        if some(3 * n + j - 1):
                            pool.wait_ge(S["rr"], 3 * n + j - 1)
                        tt(keys[:, j, :, 0:j], keys[:, j - 1, :, 0:j],
                           steps(f[:, :])[:, j][:, :, None].to_broadcast([P, CC, j]), ALU.mult).then_inc(S["rr"], 1)
                    pool.wait_ge(S["ag"], n + 1)
                    if some(3 * n):
                        pool.wait_ge(S["ap"], 3 * n)
                    tt(a[:, :], ag[:, :], f[:, :], ALU.mult).then_inc(S["a_sb"], 1)
                    pool.wait_ge(S["a_sb"], n + 1)
                    tt(feat[:, WW, :], a[:, :], feat[:, FC, :], ALU.mult).then_inc(S["wt"], 1)
                if more:
                    rest(1, n + 1, xn1, m1_1, m0_1)
                if tail:
                    pool.wait_ge(S["mix_add"], C * (d + 1))
                    if some(d):
                        pool.wait_ge(S["cenC"], d)
                    tt(o_g[:, :], uo_f[:, 1, :], og[:, d, :], ALU.mult).then_inc(S["o_g"], 1)
                if first:
                    pool.wait_ge(S["rr"], 3 * (n + 1))
                    for s in range(C):
                        tt(qp[:, n, QPAIRS[s]:QPAIRS[s] + C - s, :], steps(q[:, :])[:, s:C], keys[:, s:C, :, s],
                           ALU.mult).then_inc(S["qp"], 1)
                state_products(c, 0, SPLIT, head)
            run(pool, body)


_INS = ["L0_attn_x", "L0_attn_Wq", "L0_attn_Wk", "L0_attn_Wv", "L0_attn_Wgamma", "L0_attn_Wf1", "L0_attn_Wf2",
        "L0_attn_Wog1", "L0_attn_Wog2", "L0_attn_norm_w", "L0_attn_Wo", "L0_ffn_gate_w", "L0_ffn_w1", "L0_ffn_b1",
        "L0_ffn_w2", "L0_ffn_b2", "L0_ffn_sw1", "L0_ffn_sb1", "L0_ffn_sw2", "L0_ffn_sb2"]


def kernel(**inputs):
    import numpy as _np
    import concourse.bacc as _bacc
    from concourse import mybir as _mybir
    from concourse.bass_utils import run_bass_kernel_spmd as _run

    nc = _bacc.Bacc("TRN2", target_bir_lowering=False, num_devices=1)
    arrays, args = {}, []
    for name in _INS:
        a = _np.ascontiguousarray(inputs[name])
        arrays[f"in_{name}"] = a
        args.append(nc.dram_tensor(f"in_{name}", a.shape, _mybir.dt.from_np(a.dtype), kind="ExternalInput").ap())
    args.append(nc.dram_tensor("out_dram", (B, T, D), F32, kind="ExternalOutput").ap())
    macaron_kernel(nc, *args)
    r = _run(nc, [arrays], core_ids=[0])
    return r.results[0]["out_dram"]
```

```python
from contextlib import ExitStack

import concourse.bass as bass
from concourse import mybir

F32 = mybir.dt.float32
ALU = mybir.AluOpType
ACT = mybir.ActivationFunctionType
AX = mybir.AxisListType

P = 128
B, T, D = 4, 512, 128
H, HD = 16, 8
E, HID = 3, 512
HC = HID // P
NM = E * HC
TB = 64
NB = T // TB
N = B * TB
C = 4
NC = TB // C
CC = N // C
EPS = 1e-5
ZL = 3
SPLIT = 12
PART_STEPS = (SPLIT * C, TB - SPLIT * C)
PAIRS = (0, C - 1, 2 * C - 3)
QPAIRS = (0, C, 2 * C - 1, 3 * C - 3)
NPAIR, NQPAIR = C * (C - 1) // 2, C * (C + 1) // 2
QSPLIT = QPAIRS[2]
KH, FC, WW, QT, U0 = 3, 4, 5, 6, 7


def macaron_kernel(nc, x, Wq, Wk, Wv, Wgamma, Wf1, Wf2, Wog1, Wog2, norm_w, Wo,
                   gate_w, w1, b1, w2, b2, sw1, sb1, sw2, sb2, out):
    kfw_dram = [nc.dram_tensor(name, [NB, P, B, 3, width], F32).ap()
                for name, width in zip(("kfw_head_dram", "kfw_tail_dram"), PART_STEPS)]
    qu_dram = nc.dram_tensor("qu_dram", [NB, P, 2, B, TB], F32).ap()

    with ExitStack() as ctx:
        def sb(name, shape):
            return ctx.enter_context(nc.sbuf_tensor(name, [P] + shape, F32))

        def sem(name):
            return ctx.enter_context(nc.semaphore(name))

        ident = sb("ident", [P])
        average = sb("average", [P])
        heads = sb("heads", [P])
        w1_sb = sb("w1_sb", [E, HID])
        w2_sb = sb("w2_sb", [NM, D])
        b1_sb = sb("b1_sb", [NM])
        b2_sb = sb("b2_sb", [E])
        hb2 = sb("hb2", [1])
        gate_sb = sb("gate_sb", [2])
        gate_diff = sb("gate_diff", [1])
        gate_bc = sb("gate_bc", [P])
        wq_sb, wk_sb, wv_sb, wo_sb = (sb(n, [D]) for n in ("wq_sb", "wk_sb", "wv_sb", "wo_sb"))
        wgam_sb = sb("wgam_sb", [H])
        wgam_bc = sb("wgam_bc", [H, HD])
        wfo_sb = sb("wfo_sb", [2 * HD])
        wf2_sb = sb("wf2_sb", [D])
        wog2_sb = sb("wog2_sb", [D])
        nw_sb = sb("nw_sb", [1])

        x_in = sb("x_in", [2, D])
        x_pair = sb("x_pair", [2, N])
        xT, xn1 = x_pair[:, 0, :], x_pair[:, 1, :]
        eps = sb("eps", [1])
        stats = {t: sb("stats" + t, [2, 6]) for t in "ABCD"}
        mean_var = {t: sb("mean_var" + t, [2, 2]) for t in "ABCD"}
        sd = {t: sb("sd" + t, [2]) for t in "ABCD"}
        rsd = {t: sb("rsd" + t, [2]) for t in "ABCD"}
        shift = {t: sb("shift" + t, [2]) for t in "ABCD"}
        normed = {t: sb("normed" + t, [2, D]) for t in "ABCD"}
        xn2, xnB, onT = (sb(n, [N]) for n in ("xn2", "xnB", "onT"))
        m0_1, m1_1, m0_2, m1_2 = (sb(n, [N]) for n in ("m0_1", "m1_1", "m0_2", "m1_2"))
        hid = sb("hid", [4, N])
        y1_now = sb("y1_now", [N])
        y1T = sb("y1T", [NB, N])
        y2T = sb("y2T", [N])
        y3T = sb("y3T", [N])
        og = sb("og", [NB, N])
        sig_k, sig_q, sig_g, f = (sb(n, [N]) for n in ("sig_k", "sig_q", "sig_g", "f"))
        k_raw, k_sq, q, fo, ag, a = (sb(n, [N]) for n in ("k_raw", "k_sq", "q", "fo", "ag", "a"))
        k_wide = sb("k_wide", [2, P])
        k_floor, k_len, k_inv = (sb(n, [2, H]) for n in ("k_floor", "k_len", "k_inv"))
        feat = sb("feat", [8, N])
        ap_ = sb("ap_", [NPAIR, CC])
        qp = sb("qp", [NB, NQPAIR, CC])
        solve = sb("solve", [(C - 1) * 2 * CC])
        uo_f = sb("uo_f", [2, N])
        pairs = sb("pairs", [2, C * CC])
        o_g = sb("o_g", [N])
        y_out = sb("y_out", [2, D])

        l_kfw = [sb(name, [HD, 3, width])
                 for name, width in zip(("l_kfw_head", "l_kfw_tail"), PART_STEPS)]
        l_q = sb("l_q", [HD, TB])
        l_u0 = sb("l_u0", [HD // 2, TB])
        prod = sb("prod", [TB, HD // 2, HD + 1])
        u_l = sb("u_l", [HD // 2, TB])
        outer = sb("outer", [2, HD, HD // 2, C + 1])
        state = sb("state", [NC + 1, HD, HD // 2])
        oprod = sb("oprod", [TB, HD // 2, HD])
        osum4 = sb("osum4", [TB // 2, HD // 2, 4])
        osum2 = sb("osum2", [TB // 2, HD // 2, 2])
        uo_l = sb("uo_l", [HD // 2, 2, TB])

        bank = [ctx.enter_context(nc.psum_tensor(f"bank{i}", [P, 512], F32)) for i in range(8)]
        left, right = (lambda i: bank[i][:, 0:N]), (lambda i: bank[i][:, N:2 * N])
        p_hid = [(left, right)[m % 2](m // 2) for m in range(4)]
        p_acc = left(2)
        p_tok, p_feat = left(3), right(3)
        p_qk0, p_k, p_q = bank[4][:, 0:QSPLIT * CC], left(4), right(4)
        p_g, p_fo, p_a = left(5), bank[5][0:2 * HD, N:2 * N], bank[5][:, 0:NPAIR * CC]
        p_out, p_z2, p_v, p_n, p_kscale = left(6), left(6), left(6), bank[6][:, 0:2 * H], left(6)
        p_qk1 = bank[5][:, 0:(NQPAIR - QSPLIT) * CC]
        p_wo, p_x, p_xn, p_f, p_og, p_z1 = left(7), left(7), right(7), left(7), right(7), left(7)

        S = {}
        for name in ("w_gate", "w_up_shared", "w_up", "w_down_shared", "w_down", "w_attn", "x_in",
                     "feat_stored", "kfw_head", "kfw_tail", "u0_head", "u0_tail",
                     "q_head", "q_tail", "uo_back", "y_stored",
                     "consts_pool", "consts_dve", "consts_fold", "gate_bc", "w2_half", "setup", "setup_p", "fo_zero",
                     "xT_ps", "z_ps1", "z_ps2", "m1_1", "m1_2", "m0_1", "m0_2",
                     "up1", "up2", "relu1", "relu2", "down1", "down2",
                     "y1", "y1_kept", "y2", "y3",
                     "tokB", "tokC", "tokD", "statA", "statB", "statC", "statD",
                     "varA", "varB", "varC", "varD", "meanA", "meanB", "meanC", "meanD",
                     "sdA", "sdB", "sdC", "sdD", "rsA", "rsB", "rsC", "rsD", "normA", "normB", "normC", "normD",
                     "featB", "featC", "featD", "eps",
                     "nA", "nB", "nC", "nD",
                     "g_ps", "q_ps", "v_ps", "og_ps",
                     "sig_g", "sig_q", "fo_sb", "v_sb", "f_sb", "fc0", "og_sb",
                     "k_raw", "q_sb", "k_sq", "n_ps", "k_floor", "k_len", "k_inv", "k_wide", "k_scale", "kn",
                     "ag", "a_sb", "fc", "wt", "qt",
                     "rr", "ap", "qp", "a_ps", "fs_mul", "fs_add",
                     "u0_lane", "s0", "carried", "c_prod", "c_decay", "c_u", "c_outer", "c_state",
                     "oprod", "o_sum", "o_lane", "u_lane", "qk_ps", "mix_mul", "mix_add", "o_g", "wo_ps", "out_ps", "y_out"):
            S[name] = sem(name)

        def some(count):
            return not isinstance(count, int) or count > 0

        block = ctx.enter_context(nc.Block())

        def parts(n):
            return n < NB, 1 <= n <= NB, 2 <= n < NB + 2, ZL <= n < NB + ZL, n >= ZL + 1, n + 1 < NB

        STEADY = (ZL + 1, NB - 1)
        LAST = NB + ZL

        def run(eng, body):
            for n in range(STEADY[0]):
                body(n, *parts(n))
            with eng.Fori(STEADY[0], STEADY[1]) as n:
                body(n, *[True] * 6)
            for n in range(STEADY[1], LAST + 1):
                body(n, *parts(n))

        PV = dict(scaled_c=8, features_c=11, wo=12, tokens_d=14, deviation_d=14, features_d=18, routing=19)
        QV = dict(tokens_b=3, deviation_b=5, features_b=9, projections=12, gates=12, key_lengths=15,
                  query_pairs=15, key_scales=16)
        EV = dict(projections=1, gates=1, key_lengths=3, key_scales=7, key_pairs=14)
        DP = dict(norm_c=2, y2=11, statistics_d=14, norm_d=18, routing_2=26, y1=32, statistics_b=39)
        DQ = dict(norm_b=43, routing_1=56, key_query=64, key_floor=64, key_inverse=68, mix=69, mixed=69,
                  key_products=69, solve=74)
        ZP = dict(norm_c=10, y2=23, statistics_d=29, norm_d=30, routing_2=43, y1=56, statistics_b=58)
        ZQ = dict(norm_b=65, routing_1=81, key_query=87, key_floor=92, key_inverse=93, mix=93, mixed=98,
                  key_products=98, solve=100)
        LP = dict(norm_c=0, y2=14, statistics_d=16, norm_d=19, routing_2=32, y1=44, statistics_b=45)
        LQ = dict(norm_b=49, routing_1=51, key_query=58, key_floor=58, key_inverse=61, mix=64, mixed=67,
                  key_products=68, solve=70)
        EP = (dict(key_floor=16, key_inverse=18, normal_key=21, key_products=23, solve=36, own=45),
              dict(key_floor=21, key_inverse=25, normal_key=25, key_products=26, solve=30, own=38),
              dict(key_floor=21, key_inverse=22, normal_key=29, key_products=32, solve=37, own=53))
        EL = (dict(statistics_b=61, norm_b=61, routing_1=51, key_query=66),
              dict(statistics_b=54, norm_b=70, routing_1=73, key_query=74),
              dict(statistics_b=45, norm_b=57, routing_1=65, key_query=79))
        PP = (2, 9)

        def early_chunks(n):
            return max(0, EP[n]["own"] - 5 * (NC - SPLIT)) // 5

        def early(n):
            return isinstance(n, int) and n < ZL

        ORDER = (2, 1, 0)

        STORES = 16 * 8

        def at_most(n, top):
            return min(n, top) if isinstance(n, int) else n

        SLOTS = [("up", 0), ("up", 1)]
        for m in range(0, NM, 2):
            SLOTS += [("up", m + 2), ("up", m + 3)] if m + 2 < NM else []
            SLOTS += [("down", m), ("down", m + 1)]

        def ups(slots):
            return sum(kind == "up" for kind, _ in SLOTS[:slots]) // 2 * 2

        def steps(t, cc=CC):
            return t.rearrange("p (c j) -> p j c", j=C)

        featf = feat[:, :, :].rearrange("p a n -> p (a n)")
        key_diag = featf[:, 0:C * (N + 1)].rearrange("p (j r) -> p j r", r=N + 1)[:, :, 0:N - C + 1:C]
        keys = feat[:, 0:C, :].rearrange("p j (c s) -> p j c s", s=C)
        uw = feat[:, WW:U0 + 1:U0 - WW, :].rearrange("p x (c j) -> p x c j", j=C)

        @block.sync
        def _(sp):
            def load_x(n):
                for half in range(2):
                    src = x[2 * half:2 * half + 2, bass.ds(n * TB, TB), :]
                    sp.dma_start(x_in[:, half, :], src).then_inc(S["x_in"], 16)

            load_x(0)
            sp.dma_start(gate_sb[:, :], gate_w.rearrange("e d -> d e"), allow_slow_non_contiguous=True).then_inc(S["w_gate"], 16)
            sp.dma_start(w1_sb[:, 2, :], sw1).then_inc(S["w_up_shared"], 16)
            sp.dma_start(b1_sb[:, 2 * HC:NM], sb1.rearrange("(c p) -> p c", p=P), allow_slow_non_contiguous=True)\
              .then_inc(S["w_up_shared"], 16)
            sp.dma_start(w2_sb[:, 2 * HC:NM, :], sw2.rearrange("(c p) d -> p c d", p=P)).then_inc(S["w_down_shared"], 16)
            sp.dma_start(w1_sb[:, 0:2, :], w1.rearrange("e d h -> d e h")).then_inc(S["w_up"], 16)
            sp.dma_start(b1_sb[:, 0:2 * HC], b1.rearrange("e (c p) -> p (e c)", p=P), allow_slow_non_contiguous=True)\
              .then_inc(S["w_up"], 16)
            sp.dma_start(w2_sb[:, 0:2 * HC, :], w2.rearrange("e (c p) d -> p (e c) d", p=P)).then_inc(S["w_down"], 16)
            sp.dma_start(b2_sb[:, 0:2], b2.rearrange("e d -> d e"), allow_slow_non_contiguous=True).then_inc(S["w_down"], 16)
            sp.dma_start(b2_sb[:, 2:3], sb2.rearrange("(d a) -> d a", a=1), allow_slow_non_contiguous=True).then_inc(S["w_down"], 16)
            for dst, src in ((wq_sb, Wq), (wk_sb, Wk), (wv_sb, Wv), (wo_sb, Wo), (wgam_sb, Wgamma)):
                sp.dma_start(dst[:, :], src).then_inc(S["w_attn"], 16)
            sp.dma_start(wfo_sb[:, 0:HD], Wf1).then_inc(S["w_attn"], 16)
            sp.dma_start(wfo_sb[:, HD:2 * HD], Wog1).then_inc(S["w_attn"], 16)
            sp.wait_ge(S["fo_zero"], 2)
            sp.dma_start(wf2_sb[0:HD, :], Wf2).then_inc(S["w_attn"], 16)
            sp.dma_start(wog2_sb[HD:2 * HD, :], Wog2).then_inc(S["w_attn"], 16)
            sp.dma_start(nw_sb[:, :], norm_w.rearrange("(d a) -> d a", a=1), allow_slow_non_contiguous=True).then_inc(S["w_attn"], 16)

            sp.wait_ge(S["xT_ps"], 1)
            load_x(1)

            def load_lanes(b, lo, hi, part):
                at, end = lo * C, hi * C
                before = NC * (b - 1) + hi
                if some(before):
                    sp.wait_ge(S["c_state"], before)
                for vh in range(2):
                    sp.dma_start(l_kfw[part][64 * vh:64 * vh + 64, :, :, :],
                                 kfw_dram[part][b].rearrange("(h k) b a t -> b h k (a t)", k=HD))\
                      .then_inc(S[("kfw_head", "kfw_tail")[part]], 16)
                if some(2 * b - 1 + part):
                    sp.wait_ge(S["u0_lane"], 2 * b - 1 + part)
                for vh in range(2):
                    sp.dma_start(l_u0[64 * vh:64 * vh + 64, :, at:end],
                                 qu_dram[b][:, 1, :, at:end].rearrange("(h v g) b t -> g b h v t", v=HD // 2, g=2)[vh])\
                      .then_inc(S[("u0_head", "u0_tail")[part]], 16)
                if some(before):
                    sp.wait_ge(S["oprod"], before)
                for vh in range(2):
                    sp.dma_start(l_q[64 * vh:64 * vh + 64, :, at:end],
                                 qu_dram[b][:, 0, :, at:end].rearrange("(h k) b t -> b h k t", k=HD))\
                      .then_inc(S[("q_head", "q_tail")[part]], 16)

            def store_lanes(b, array, slot):
                src = feat[:, slot, :].rearrange("p (b t) -> p b t", t=TB)
                for part, at in ((0, 0), (1, SPLIT * C)):
                    sp.dma_start(kfw_dram[part][b][:, :, array], src[:, :, at:at + PART_STEPS[part]])\
                      .then_inc(S["feat_stored"], 16)

            def body(n, first, head, tail, second, store, more):
                c, d, t = n - 1, n - 2, n - ZL - 1
                if head:
                    sp.wait_ge(S["feat_stored"], STORES * (c + 1))
                    load_lanes(c, 0, SPLIT, 0)
                if store:
                    sp.wait_ge(S["y_out"], t + 1)
                    for half in range(2):
                        sp.dma_start(out[2 * half:2 * half + 2, bass.ds(t * TB, TB), :],
                                     y_out[:, half, :]).then_inc(S["y_stored"], 16)
                if tail:
                    sp.wait_ge(S["u_lane"], d + 1)
                    sp.wait_ge(S["o_lane"], 2 * (d + 1))
                    if some(d):
                        sp.wait_ge(S["mix_add"], C * d)
                        sp.wait_ge(S["o_g"], d)
                    for vh in range(2):
                        for b in range(B):
                            sp.dma_start(uo_f[vh:P:2, :, TB * b:TB * b + TB],
                                         uo_l[64 * vh + H * b:64 * vh + H * b + H, :, :, :]).then_inc(S["uo_back"], 16)
                if head:
                    load_lanes(c, SPLIT, NC, 1)
                if n + 2 < NB:
                    sp.wait_ge(S["xT_ps"], n + 2)
                    load_x(n + 2)
                if first:
                    sp.wait_ge(S["fc"], 3 * (n + 1))
                    store_lanes(n, 1, FC)
                    sp.wait_ge(S["qt"], n + 1)
                    sp.dma_start(qu_dram[n][:, 0].rearrange("p b t -> p (b t)"), feat[:, QT, :]).then_inc(S["feat_stored"], 16)
                    sp.wait_ge(S["rr"], 3 * (n + 1))
                    store_lanes(n, 0, KH)
                    sp.wait_ge(S["fs_add"], 3 * (n + 1))
                    store_lanes(n, 2, WW)
                    sp.dma_start(qu_dram[n][:, 1].rearrange("p b t -> p (b t)"), feat[:, U0, :]).then_inc(S["feat_stored"], 16)
            for n in range(LAST + 1):
                body(n, *parts(n))
            sp.wait_ge(S["y_stored"], 32 * NB + 1)

        @block.tensor
        def _(pe):
            mm = nc.tensor.matmul

            def slot(tag, b, i):
                kind, m = SLOTS[i]
                e, w = ORDER[m // HC], ORDER[m // HC] * HC + m % HC
                if kind == "up":
                    if tag == 1 and isinstance(b, int) and b == 0:
                        if m == 0:
                            pe.wait_ge(S["w_up_shared"], 16 * 2)
                        if m == HC:
                            pe.wait_ge(S["w_up"], 16 * 2)
                    if m == 0:
                        pe.wait_ge(S[("nA", "nD")[tag - 1]], b + 1)
                    if m == HC:
                        pe.wait_ge(S[f"m1_{tag}"], b + 1)
                    if m == 2 * HC:
                        pe.wait_ge(S[f"m0_{tag}"], b + 1)
                    if m in (0, 2):
                        other = (b - ZL, at_most(b + ZL + 1, NB))[tag - 1]
                        if some(NM * other - 2 + m):
                            pe.wait_ge(S[f"relu{3 - tag}"], NM * other - 2 + m)
                    if m % 2 == 0:
                        if some(NM * b + m - 2):
                            pe.wait_ge(S[f"relu{tag}"], NM * b + m - 2)
                    src = {2: (xn1, xn2), 1: (m1_1, m1_2), 0: (m0_1, m0_2)}[e][tag - 1]
                    mm(p_hid[m % 4], w1_sb[:, e, P * (m % HC):P * (m % HC) + P], src[:, :],
                       start=True, stop=True).then_inc(S[f"up{tag}"], 1)
                else:
                    if tag == 1 and isinstance(b, int) and b == 0 and m in (0, HC):
                        pe.wait_ge(S["w2_half"], 1 + (m > 0))
                    if m == 0:
                        if some(b):
                            pe.wait_ge(S[("y1", "y3")[tag - 1]], b)
                        if some((b - ZL, at_most(b + ZL + 1, NB))[tag - 1]):
                            pe.wait_ge(S[("y3", "y1")[tag - 1]], (b - ZL, at_most(b + ZL + 1, NB))[tag - 1])
                    pe.wait_ge(S[f"relu{tag}"], NM * b + m + 1)
                    mm(p_acc, w2_sb[:, w, :], hid[:, m % 4, :], start=m == 0, stop=m == NM - 1)\
                        .then_inc(S[f"down{tag}"], 1)

            def ffn(tag, b, lo, hi, there):
                if there:
                    for i in range(lo, hi):
                        slot(tag, b, i)

            def transposed_in(b):
                pe.wait_ge(S["x_in"], 32 * (b + 1))
                if some(b):
                    pe.wait_ge(S["m1_1"], b)
                if some(b - 1):
                    pe.wait_ge(S["og_sb"], b - 1)
                pe.wait_ge(S["normA"], b + 1)
                for half in range(2):
                    nc.tensor.transpose(p_x[:, P * half:P * half + P], x_in[:, half, :], ident[:, :])
                    last = nc.tensor.transpose(p_xn[:, P * half:P * half + P], normed["A"][:, half, :], ident[:, :])
                last.then_inc(S["xT_ps"], 1)

            def to_tokens(tag, b, src, ready):
                pe.wait_ge(S[ready], b + 1)
                for half in range(2):
                    last = nc.tensor.transpose(p_tok[:, P * half:P * half + P], src[:, P * half:P * half + P], ident[:, :])
                last.then_inc(S["tok" + tag], 1)

            def to_features(tag, b):
                pe.wait_ge(S["norm" + tag], b + 1)
                for half in range(2):
                    last = nc.tensor.transpose(p_feat[:, P * half:P * half + P], normed[tag][:, half, :], ident[:, :])
                last.then_inc(S["feat" + tag], 1)

            def routed(tag, b, src):
                pe.wait_ge(S[("nA", "nD")[tag - 1]], b + 1)
                mm((p_z1, p_z2)[tag - 1], gate_bc[:, :], src[:, :], start=True, stop=True).then_inc(S[f"z_ps{tag}"], 1)

            pe.wait_ge(S["setup_p"], 2)
            transposed_in(0)
            pe.wait_ge(S["gate_bc"], 1)
            routed(1, 0, xn1)

            def projections(n, z, second):
                pe.wait_ge(S["nB"], n + 1)
                if isinstance(n, int) and n == 0:
                    pe.wait_ge(S["w_attn"], 16 * 10)
                    pe.wait_ge(S["setup"], 3)
                if some(3 * n):
                    pe.wait_ge(S["fs_mul"], 3 * n)
                if some(C * (n - 2)):
                    pe.wait_ge(S["mix_mul"], C * (n - 2))
                mm(p_fo, wfo_sb[:, :], xnB[:, :], start=True, stop=True)
                mm(p_g, wgam_bc[:, :, :], xnB[:, :], start=True, stop=True).then_inc(S["g_ps"], 1)
                if some(n):
                    pe.wait_ge(S["q_sb"], n)
                mm(p_k, wk_sb[:, :], xnB[:, :], start=True, stop=True)
                mm(p_q, wq_sb[:, :], xnB[:, :], start=True, stop=True).then_inc(S["q_ps"], 1)
                if some(n):
                    pe.wait_ge(S["kn"], n)
                if second:
                    pe.wait_ge(S["m1_2"], z + 1)
                mm(p_v, wv_sb[:, :], xnB[:, :], start=True, stop=True).then_inc(S["v_ps"], 1)

            def gates(n, z, second, x_read, routed_blocks):
                pe.wait_ge(S["fo_sb"], n + 1)
                pe.wait_ge(S["m1_1"], routed_blocks)
                if second:
                    pe.wait_ge(S["y2"], z + 1)
                pe.wait_ge(S["nA"], x_read)
                mm(p_f, wf2_sb[0:2 * HD, :], fo[0:2 * HD, :], start=True, stop=True)
                mm(p_og, wog2_sb[0:2 * HD, :], fo[0:2 * HD, :], start=True, stop=True).then_inc(S["og_ps"], 1)

            def key_lengths(n):
                pe.wait_ge(S["k_sq"], n + 1)
                pe.wait_ge(S["v_sb"], n + 1)
                for half in range(2):
                    last = mm(p_n[:, H * half:H * half + H], k_sq[:, P * half:P * half + P], heads[:, 0:P:HD],
                              start=True, stop=True)
                last.then_inc(S["n_ps"], 1)

            def key_scales(n):
                pe.wait_ge(S["k_wide"], n + 1)
                for half in range(2):
                    last = mm(p_kscale[:, P * half:P * half + P], k_wide[:, half, :], ident[:, :], start=True, stop=True)
                last.then_inc(S["k_scale"], 1)

            def query_pairs(d, projected, solved):
                pe.wait_ge(S["qp"], C * (d + 1))
                if some(C * d):
                    pe.wait_ge(S["mix_mul"], C * d)
                pe.wait_ge(S["q_sb"], projected)
                pe.wait_ge(S["sig_g"], projected)
                mm(p_qk0, heads[:, :], qp[:, d, 0:QSPLIT, :], start=True, stop=True)
                pe.wait_ge(S["fs_mul"], 3 * solved)
                mm(p_qk1, heads[:, :], qp[:, d, QSPLIT:NQPAIR, :], start=True, stop=True).then_inc(S["qk_ps"], 1)

            def head_norm(n, d):
                pe.wait_ge(S["nB"], at_most(n + 1, NB))
                if some(at_most(d, NB)):
                    pe.wait_ge(S["nD"], d)
                to_tokens("C", d, o_g[:, :], "o_g")

            def key_pairs(n, mixed):
                pe.wait_ge(S["ap"], 3 * (n + 1))
                if some(C * mixed):
                    pe.wait_ge(S["mix_mul"], C * mixed)
                pe.wait_ge(S["sig_g"], n + 1)
                mm(p_a, heads[:, :], ap_[:, :, :], start=True, stop=True).then_inc(S["a_ps"], 1)

            def body(n, first, head, tail, second, store, more):
                d, z, t = n - 2, n - ZL, n - ZL - 1
                here = first and not (isinstance(n, int) and 1 <= n <= ZL)
                ffn(1, n, 0, 2, here)
                ffn(1, n, 2, 4, here)
                if store:
                    pe.wait_ge(S["y3"], t + 1)
                    if some(at_most(n, NB)):
                        pe.wait_ge(S["kn"], at_most(n, NB))
                    pe.wait_ge(S["m1_2"], z)
                    for half in range(2):
                        last = nc.tensor.transpose(p_out[:, P * half:P * half + P], y3T[:, P * half:P * half + P], ident[:, :])
                    last.then_inc(S["out_ps"], 1)
                ffn(1, n, 4, PV["scaled_c"], here)
                ffn(1, n, PV["scaled_c"], PV["features_c"], here)
                if second:
                    to_features("C", z)
                ffn(1, n, PV["features_c"], PV["wo"], here)
                if second:
                    pe.wait_ge(S["nC"], z + 1)
                    pe.wait_ge(S["m1_1"], at_most(n + 1, NB))
                    if some(z):
                        pe.wait_ge(S["y2"], z)
                    mm(p_wo, wo_sb[:, :], onT[:, :], start=True, stop=True).then_inc(S["wo_ps"], 1)
                ffn(1, n, PV["wo"], PV["tokens_d"], here)
                if second:
                    pe.wait_ge(S["nC"], z + 1)
                    to_tokens("D", z, y2T[:, :], "y2")
                ffn(1, n, PV["tokens_d"], PV["deviation_d"], here)
                ffn(1, n, PV["deviation_d"], PV["features_d"], here)
                if second:
                    to_features("D", z)
                ffn(1, n, PV["features_d"], PV["routing"], here)
                if second:
                    if some(z):
                        pe.wait_ge(S["y_out"], z)
                    pe.wait_ge(S["kn"], at_most(n, NB))
                    routed(2, z, xn2)
                ffn(1, n, PV["routing"], 24, here)

                if early(n):
                    if some(n):
                        pe.wait_ge(S["nB"], n)
                    to_tokens("B", n, y1_now[:, :], "y1")
                    transposed_in(n + 1)
                    routed(1, n + 1, xn1)
                    to_features("B", n)
                    ffn(1, n + 1, 0, EV["projections"], True)
                    projections(n, z, False)
                    ffn(1, n + 1, EV["projections"], EV["gates"], True)
                    gates(n, z, False, n + 2, n + 2)
                    ffn(1, n + 1, EV["gates"], EV["key_lengths"], True)
                    key_lengths(n)
                    ffn(1, n + 1, EV["key_lengths"], EV["key_scales"], True)
                    key_scales(n)
                    ffn(1, n + 1, EV["key_scales"], EV["key_pairs"], True)
                    key_pairs(n, 0)
                    ffn(1, n + 1, EV["key_pairs"], 24, True)
                    if tail:
                        query_pairs(d, n + 1, n + 1)
                        head_norm(n, d)
                    return
                if tail and not first:
                    query_pairs(d, NB, NB)
                ffn(2, z, 0, QV["tokens_b"], second)
                if first:
                    if some(n):
                        pe.wait_ge(S["nB"], n)
                    pe.wait_ge(S["nD"], z + 1)
                    to_tokens("B", n, y1_now[:, :], "y1")
                if more:
                    pe.wait_ge(S["y2"], z + 1)
                    transposed_in(n + 1)
                ffn(2, z, QV["tokens_b"], QV["deviation_b"], second)
                if more:
                    routed(1, n + 1, xn1)
                ffn(2, z, QV["deviation_b"], QV["features_b"], second)
                if first:
                    to_features("B", n)
                ffn(2, z, QV["features_b"], QV["projections"], second)
                if first:
                    projections(n, z, True)
                ffn(2, z, QV["projections"], QV["gates"], second)
                if first:
                    gates(n, z, True, at_most(n + 2, NB), at_most(n + 2, NB))
                ffn(2, z, QV["gates"], QV["key_lengths"], second)
                if first:
                    key_lengths(n)
                ffn(2, z, QV["key_lengths"], QV["query_pairs"], second)
                if first:
                    query_pairs(d, n + 1, n)
                ffn(2, z, QV["query_pairs"], QV["key_scales"], second)
                if first:
                    key_scales(n)
                ffn(2, z, QV["key_scales"], 24, second)
                if tail:
                    head_norm(n, d)
                if first:
                    key_pairs(n, n - 1)
            run(pe, body)

        @block.scalar
        def _(act):
            def relu(tag, b, lo, hi, there):
                if there:
                    for m in range(ups(lo), ups(hi)):
                        w = ORDER[m // HC] * HC + m % HC
                        if tag == 1 and isinstance(b, int) and b == 0 and m in (0, HC):
                            act.wait_ge(S[("w_up_shared", "w_up")[m > 0]], 16 * 2)
                        act.wait_ge(S[f"up{tag}"], NM * b + m // 2 * 2 + 2)
                        if m < 4:
                            other = (b - ZL, at_most(b + ZL + 1, NB))[tag - 1]
                            if some(NM * other - 3 + m):
                                act.wait_ge(S[f"down{3 - tag}"], NM * other - 3 + m)
                        if some(NM * b + m - 3):
                            act.wait_ge(S[f"down{tag}"], NM * b + m - 3)
                        nc.scalar.activation(hid[:, m % 4, :], p_hid[m % 4], ACT.Relu, bias=b1_sb[:, w:w + 1])\
                            .then_inc(S[f"relu{tag}"], 1)

            def deviation(tag, b):
                act.wait_ge(S["var" + tag], b + 1)
                nc.scalar.activation(sd[tag][:, :], mean_var[tag][:, :, 1], ACT.Sqrt, bias=eps[:, :]).then_inc(S["sd" + tag], 1)

            def scaled(tag, b):
                src = x_in[:, :, :] if tag == "A" else p_tok.rearrange("p (h d) -> p h d", h=2)
                act.wait_ge(S["mean" + tag], b + 1)
                if tag == "A":
                    act.wait_ge(S["x_in"], 32 * (b + 1))
                if some(b):
                    act.wait_ge(S["nA" if tag == "A" else "feat" + tag], b)
                for half in range(2):
                    last = nc.scalar.activation(normed[tag][:, half, :], src[:, half, :], ACT.Identity,
                                                bias=shift[tag][:, half:half + 1], scale=rsd[tag][:, half:half + 1])
                last.then_inc(S["norm" + tag], 1)

            def normalised(tag, b, dst):
                act.wait_ge(S["feat" + tag], b + 1)
                nc.scalar.copy(dst[:, :], p_feat).then_inc(S["n" + tag], 1)

            def x_copy(b):
                act.wait_ge(S["xT_ps"], b + 1)
                if some(b):
                    act.wait_ge(S["y1"], b)
                nc.scalar.copy(x_pair[:, :, :], bank[7].rearrange("p (a n) -> p a n", a=2)).then_inc(S["nA"], 1)

            act.wait_ge(S["eps"], 1)
            deviation("A", 0)
            scaled("A", 0)
            x_copy(0)

            def keep_y1(n):
                act.wait_ge(S["y1"], n + 1)
                nc.scalar.copy(y1T[:, n, :], y1_now[:, :]).then_inc(S["y1_kept"], 1)

            def gate_inputs(n):
                act.wait_ge(S["g_ps"], n + 1)
                nc.scalar.copy(fo[0:2 * HD, :], p_fo).then_inc(S["fo_sb"], 1)
                act.wait_ge(S["q_ps"], n + 1)
                if some(n):
                    act.wait_ge(S["k_raw"], n)
                nc.scalar.activation(sig_k[:, :], p_k, ACT.Sigmoid)
                if some(n):
                    act.wait_ge(S["q_sb"], n)
                nc.scalar.activation(sig_q[:, :], p_q, ACT.Sigmoid).then_inc(S["sig_q"], 1)
                if some(n):
                    act.wait_ge(S["ag"], n)
                nc.scalar.activation(sig_g[:, :], p_g, ACT.Sigmoid).then_inc(S["sig_g"], 1)
                act.wait_ge(S["v_ps"], n + 1)
                if some(n):
                    act.wait_ge(S["feat_stored"], STORES * n)
                nc.scalar.copy(feat[:, U0, :], p_v).then_inc(S["v_sb"], 1)

            def gates(n):
                act.wait_ge(S["og_ps"], n + 1)
                if some(3 * n):
                    act.wait_ge(S["rr"], 3 * n)
                if some(n):
                    act.wait_ge(S["a_sb"], n)
                nc.scalar.activation(f[:, :], p_f, ACT.Sigmoid).then_inc(S["f_sb"], 1)
                nc.scalar.activation(steps(feat[:, FC, :])[:, 0], steps(p_f)[:, 0], ACT.Sigmoid).then_inc(S["fc0"], 1)
                act.wait_ge(S["k_raw"], n + 1)
                nc.scalar.activation(k_sq[:, :], k_raw[:, :], ACT.Square).then_inc(S["k_sq"], 1)
                nc.scalar.activation(og[:, n, :], p_og, ACT.Sigmoid).then_inc(S["og_sb"], 1)

            def key_length(n):
                act.wait_ge(S["k_floor"], n + 1)
                nc.scalar.activation(k_len[:, :, :], k_floor[:, :, :], ACT.Sqrt).then_inc(S["k_len"], 1)

            def key_scale(n):
                act.wait_ge(S["k_inv"], n + 1)
                nc.scalar.copy(k_wide[:, :, :].rearrange("p a (h k) -> p a h k", k=HD),
                               k_inv[:, :, :, None].to_broadcast([P, 2, H, HD])).then_inc(S["k_wide"], 1)

            def body(n, first, head, tail, second, store, more):
                z, t = n - ZL, n - ZL - 1
                here = first and not (isinstance(n, int) and 1 <= n <= ZL)
                relu(1, n, 0, 2, here)
                relu(1, n, 2, 4, here)
                if store:
                    act.wait_ge(S["out_ps"], t + 1)
                    act.wait_ge(S["y_stored"], 32 * t + 1)
                    nc.scalar.copy(y_out[:, :, :], p_out.rearrange("p (h d) -> p h d", h=2)).then_inc(S["y_out"], 1)
                relu(1, n, 4, PV["scaled_c"], here)
                if second:
                    scaled("C", z)
                relu(1, n, PV["scaled_c"], PV["features_c"], here)
                if second:
                    normalised("C", z, onT)
                relu(1, n, PV["features_c"], PV["deviation_d"], here)
                if second:
                    deviation("D", z)
                relu(1, n, PV["deviation_d"], (PV["deviation_d"] + PV["features_d"]) // 2, here)
                if second:
                    scaled("D", z)
                relu(1, n, (PV["deviation_d"] + PV["features_d"]) // 2, PV["features_d"], here)
                if second:
                    normalised("D", z, xn2)
                if more:
                    deviation("A", n + 1)
                relu(1, n, PV["features_d"], 24, here)
                if more:
                    scaled("A", n + 1)

                if early(n):
                    x_copy(n + 1)
                    deviation("B", n)
                    keep_y1(n)
                    scaled("B", n)
                    normalised("B", n, xnB)
                    relu(1, n + 1, 0, EV["projections"], True)
                    gate_inputs(n)
                    relu(1, n + 1, EV["projections"], EV["gates"], True)
                    gates(n)
                    relu(1, n + 1, EV["gates"], EV["key_lengths"], True)
                    key_length(n)
                    relu(1, n + 1, EV["key_lengths"], EV["key_scales"], True)
                    key_scale(n)
                    relu(1, n + 1, EV["key_scales"], 24, True)
                    if tail:
                        deviation("C", n - 2)
                    return
                relu(2, z, 0, QV["tokens_b"], second)
                if more:
                    x_copy(n + 1)
                relu(2, z, QV["tokens_b"], QV["deviation_b"], second)
                if first:
                    deviation("B", n)
                    keep_y1(n)
                relu(2, z, QV["deviation_b"], (QV["deviation_b"] + QV["features_b"]) // 2, second)
                if first:
                    scaled("B", n)
                relu(2, z, (QV["deviation_b"] + QV["features_b"]) // 2, QV["features_b"], second)
                if first:
                    normalised("B", n, xnB)
                relu(2, z, QV["features_b"], QV["projections"], second)
                if first:
                    gate_inputs(n)
                relu(2, z, QV["projections"], QV["gates"], second)
                if first:
                    gates(n)
                relu(2, z, QV["gates"], QV["key_lengths"], second)
                if first:
                    key_length(n)
                relu(2, z, QV["key_lengths"], QV["query_pairs"], second)
                if first:
                    key_scale(n)
                relu(2, z, QV["query_pairs"], 24, second)
                if tail:
                    deviation("C", n - 2)
            run(act, body)

        @block.vector
        def _(dve):
            tt, ts, stt = nc.vector.tensor_tensor, nc.vector.tensor_scalar, nc.vector.scalar_tensor_tensor

            nc.vector.memset(wf2_sb[0:2 * HD, :], 0.0).then_inc(S["fo_zero"], 1)
            nc.vector.memset(wog2_sb[0:2 * HD, :], 0.0).then_inc(S["fo_zero"], 1)
            nc.vector.memset(eps[:, :], EPS).then_inc(S["eps"], 1)
            nc.vector.memset(y_out[:, :, :], 0.0).then_inc(S["y_stored"], 1)
            nc.vector.memset(state[:, NC, :, :], 0.0).then_inc(S["s0"], 1)
            dve.wait_ge(S["w_gate"], 16)
            tt(gate_diff[:, :], gate_sb[:, 1:2], gate_sb[:, 0:1], ALU.subtract).then_inc(S["consts_dve"], 1)
            dve.wait_ge(S["consts_dve"], 1)
            dve.wait_ge(S["consts_pool"], 2)
            ts(gate_bc[:, :], average[:, :], 0.0, gate_diff[:, :], ALU.mult, ALU.add).then_inc(S["gate_bc"], 1)

            position, end, before = [0], [0], [0]
            issue = [None]

            def upto(count):
                while position[0] < min(count, end[0]):
                    issue[0](position[0])
                    position[0] += 1
                while position[0] < end[0] and (position[0] - before[0]) % 5 in (1, 2):
                    issue[0](position[0])
                    position[0] += 1

            def fill():
                upto(position[0] + 1)

            def statistics(tag, b):
                dve.wait_ge(S["x_in" if tag == "A" else "tok" + tag], (32 if tag == "A" else 1) * (b + 1))
                src = x_in[:, :, :] if tag == "A" else p_tok.rearrange("p (h d) -> p h d", h=2)
                if some(b):
                    dve.wait_ge(S["var" + tag], b)
                for half in range(2):
                    last = nc.vector.bn_stats(stats[tag][:, half, :], src[:, half, :])
                last.then_inc(S["stat" + tag], 1)
                fill()
                dve.wait_ge(S["eps"], 1)
                dve.wait_ge(S["stat" + tag], b + 1)
                if some(b):
                    dve.wait_ge(S["norm" + tag], b)
                for half in range(2):
                    last = nc.vector.bn_aggr(mean_var[tag][:, half, :], stats[tag][:, half, :])
                last.then_inc(S["var" + tag], 1)

            def normalised(tag, b):
                dve.wait_ge(S["sd" + tag], b + 1)
                if some(b):
                    dve.wait_ge(S["norm" + tag], b)
                nc.vector.reciprocal(rsd[tag][:, :], sd[tag][:, :]).then_inc(S["rs" + tag], 1)
                fill()
                dve.wait_ge(S["rs" + tag], b + 1)
                stt(shift[tag][:, :], mean_var[tag][:, :, 0], -1.0, rsd[tag][:, :], ALU.mult, ALU.mult)\
                    .then_inc(S["mean" + tag], 1)

            def routing(tag, b, src, dst):
                dve.wait_ge(S[f"z_ps{tag}"], b + 1)
                stt(dst[:, :], (p_z1, p_z2)[tag - 1], 0.0, src[:, :], ALU.is_gt, ALU.mult).then_inc(S[f"m1_{tag}"], 1)

            statistics("A", 0)
            normalised("A", 0)
            routing(1, 0, xn1, m1_1)

            dve.wait_ge(S["w_down_shared"], 16)
            ts(w2_sb[:, 2 * HC:NM, :], w2_sb[:, 2 * HC:NM, :], 0.5, None, ALU.mult).then_inc(S["w2_half"], 1)
            dve.wait_ge(S["w_down"], 16 * 3)
            ts(w2_sb[:, 0:2 * HC, :], w2_sb[:, 0:2 * HC, :], 0.5, None, ALU.mult).then_inc(S["w2_half"], 1)
            nc.vector.tensor_reduce(hb2[:, :], b2_sb[:, :], axis=AX.X, op=ALU.add).then_inc(S["consts_dve"], 1)
            dve.wait_ge(S["consts_dve"], 2)
            ts(hb2[:, :], hb2[:, :], 0.5, None, ALU.mult).then_inc(S["setup"], 1)
            dve.wait_ge(S["w_attn"], 16 * 10)
            ts(wo_sb[:, :], wo_sb[:, :], nw_sb[:, :], None, ALU.mult).then_inc(S["setup"], 1)
            nc.vector.tensor_copy(wgam_bc[:, :, :], wgam_sb[:, :, None].to_broadcast([P, H, HD])).then_inc(S["setup"], 1)
            dve.wait_ge(S["setup"], 3)

            def scan_op(b, i):
                c, kind = divmod(i, 5)
                done = NC * b + c
                steps_c = slice(C * c, C * c + C)
                lanes = l_kfw[c >= SPLIT]
                first_step = C * (c - SPLIT * (c >= SPLIT))
                lanes_c = slice(first_step, first_step + C)
                now, nxt = c, c + 1
                if kind == 0:
                    if c in (0, SPLIT):
                        part, part_end = ((0, SPLIT), (1, NC))[c > 0]
                        part_steps = slice(C * c, C * part_end)
                        dve.wait_ge(S[("u0_head", "u0_tail")[part]], 32 * (b + 1))
                        if some(NC * (b - 1) + part_end):
                            dve.wait_ge(S["c_u"], NC * (b - 1) + part_end)
                        nc.vector.tensor_copy(prod[:, part_steps, :, HD], l_u0[:, :, part_steps].rearrange("p v t -> p t v"))\
                            .then_inc(S["u0_lane"], 1)
                        if some(NC * (b - 1) + part_end):
                            dve.wait_ge(S["oprod"], NC * (b - 1) + part_end)
                        if c == 0:
                            if some(b):
                                dve.wait_ge(S["oprod"], NC * (b - 1) + SPLIT + 1)
                                dve.wait_ge(S["c_state"], NC * b)
                            dve.wait_ge(S["s0"], 1)
                            nc.vector.tensor_copy(state[:, 0], state[:, NC]).then_inc(S["carried"], 1)
                            dve.wait_ge(S["carried"], b + 1)
                        dve.wait_ge(S[("kfw_head", "kfw_tail")[part]], 32 * (b + 1))
                    if some(done):
                        dve.wait_ge(S["c_state"], done)
                    tt(prod[:, steps_c, :, 0:HD],
                       lanes[:, :, 2, lanes_c].rearrange("p k j -> p j k")[:, :, None, :].to_broadcast([P, C, HD // 2, HD]),
                       state[:, now].rearrange("p k v -> p v k")[:, None].to_broadcast([P, C, HD // 2, HD]),
                       ALU.mult).then_inc(S["c_prod"], 1)
                elif kind == 1:
                    tt(outer[:, c % 2, :, :, C],
                       lanes[:, :, 1, first_step + C - 1][:, :, None].to_broadcast([P, HD, HD // 2]),
                       state[:, now], ALU.mult).then_inc(S["c_decay"], 1)
                elif kind == 2:
                    if c in (0, SPLIT):
                        dve.wait_ge(S["u0_lane"], 2 * b + 1 + (c > 0))
                    if c == 0:
                        if some(b):
                            dve.wait_ge(S["u_lane"], b)
                    dve.wait_ge(S["c_prod"], done + 1)
                    nc.vector.tensor_reduce(u_l[:, :, steps_c].rearrange("p v j -> p j v"), prod[:, steps_c],
                                            axis=AX.X, op=ALU.add).then_inc(S["c_u"], 1)
                elif kind == 3:
                    dve.wait_ge(S["c_u"], done + 1)
                    tt(outer[:, c % 2, :, :, 0:C],
                       lanes[:, :, 0, lanes_c][:, :, None, :].to_broadcast([P, HD, HD // 2, C]),
                       u_l[:, :, steps_c][:, None].to_broadcast([P, HD, HD // 2, C]),
                       ALU.mult).then_inc(S["c_outer"], 1)
                else:
                    dve.wait_ge(S["c_decay"], done + 1)
                    dve.wait_ge(S["c_outer"], done + 1)
                    nc.vector.tensor_reduce(state[:, nxt], outer[:, c % 2], axis=AX.X, op=ALU.add)\
                        .then_inc(S["c_state"], 1)

            def mix(b, s):
                if s == 0:
                    dve.wait_ge(S["qk_ps"], b + 1)
                    dve.wait_ge(S["uo_back"], 16 * 8 * (b + 1))
                width = (C - s) * CC
                pair = (p_qk0 if s < 2 else p_qk1)
                at = (QPAIRS[s] - (0 if s < 2 else QSPLIT)) * CC
                if some(C * b + s - 1):
                    dve.wait_ge(S["mix_add"], C * b + s - 1)
                tt(pairs[:, s % 2, 0:width].rearrange("p (j c) -> p j c", c=CC),
                   pair[:, at:at + width].rearrange("p (j c) -> p j c", c=CC),
                   steps(uo_f[:, 0, :])[:, s][:, None].to_broadcast([P, C - s, CC]), ALU.mult).then_inc(S["mix_mul"], 1)

            def mixed(b, s):
                width = (C - s) * CC
                dve.wait_ge(S["mix_mul"], C * b + s + 1)
                if some(C * b + s):
                    dve.wait_ge(S["mix_add"], C * b + s)
                tt(steps(uo_f[:, 1, :])[:, s:C], pairs[:, s % 2, 0:width].rearrange("p (j c) -> p j c", c=CC),
                   steps(uo_f[:, 1, :])[:, s:C], ALU.add).then_inc(S["mix_add"], 1)

            def recurrence(c, lo, hi, head, tail):
                rest_ops = 5 * (NC - SPLIT)
                for i in range(lo, hi):
                    if i < rest_ops and tail:
                        scan_op(c - 1, 5 * SPLIT + i)
                    if i == rest_ops - 1 and tail:
                        u_output(c - 1)
                    if i >= rest_ops and head:
                        scan_op(c, i - rest_ops)

            def u_output(b):
                dve.wait_ge(S["c_u"], NC * (b + 1))
                if some(16 * 8 * b):
                    dve.wait_ge(S["uo_back"], 16 * 8 * b)
                nc.vector.tensor_copy(uo_l[:, :, 0, :], u_l[:, :, :]).then_inc(S["u_lane"], 1)

            def first_sum(n):
                dve.wait_ge(S["down1"], NM * (n + 1))
                if some(n):
                    dve.wait_ge(S["y1_kept"], n)
                    dve.wait_ge(S["tokB"], n)
                stt(y1_now[:, :], p_acc, hb2[:, :], xT[:, :], ALU.add, ALU.add).then_inc(S["y1"], 1)

            def key_and_query(n):
                dve.wait_ge(S["sig_q"], n + 1)
                tt(k_raw[:, :], p_k, sig_k[:, :], ALU.mult).then_inc(S["k_raw"], 1)
                if some(n):
                    dve.wait_ge(S["qt"], n)
                    dve.wait_ge(S["qp"], C * n)
                tt(q[:, :], p_q, sig_q[:, :], ALU.mult).then_inc(S["q_sb"], 1)

            def key_floor(n):
                dve.wait_ge(S["n_ps"], n + 1)
                ts(k_floor[:, :, :], p_n.rearrange("p (a h) -> p a h", a=2), 1e-24, None, ALU.max).then_inc(S["k_floor"], 1)

            def key_inverse(n):
                dve.wait_ge(S["k_len"], n + 1)
                nc.vector.reciprocal(k_inv[:, :, :], k_len[:, :, :]).then_inc(S["k_inv"], 1)

            def normal_key(n):
                dve.wait_ge(S["k_scale"], n + 1)
                if some(n):
                    dve.wait_ge(S["qp"], C * n)
                    dve.wait_ge(S["feat_stored"], STORES * n)
                tt(key_diag, steps(k_raw[:, :]), steps(p_kscale), ALU.mult).then_inc(S["kn"], 1)

            def key_gamma(n):
                dve.wait_ge(S["kn"], n + 1)
                dve.wait_ge(S["sig_g"], n + 1)
                if some(n):
                    dve.wait_ge(S["a_sb"], n)
                stt(steps(ag[:, :]), key_diag, -1.0, steps(sig_g[:, :]), ALU.mult, ALU.mult).then_inc(S["ag"], 1)

            def key_products(n):
                dve.wait_ge(S["rr"], 3 * (n + 1))
                dve.wait_ge(S["a_sb"], n + 1)
                for s in range(C - 1):
                    tt(ap_[:, PAIRS[s]:PAIRS[s] + C - 1 - s, :], steps(a[:, :])[:, s + 1:C], keys[:, s + 1:C, :, s],
                       ALU.mult).then_inc(S["ap"], 1)
                    if s < C - 2:
                        fill()

            def substitution(n):
                dve.wait_ge(S["a_ps"], n + 1)
                dve.wait_ge(S["wt"], n + 1)
                dve.wait_ge(S["v_sb"], n + 1)
                for s in range(C - 1):
                    left = C - 1 - s
                    tmp = solve[:, 0:left * 2 * CC].rearrange("p (j x c) -> p j x c", x=2, c=CC)
                    if some(3 * n + s):
                        dve.wait_ge(S["fs_add"], 3 * n + s)
                    tt(tmp, p_a.rearrange("p (j c) -> p j c", c=CC)[:, PAIRS[s]:PAIRS[s] + left][:, :, None]
                       .to_broadcast([P, left, 2, CC]),
                       uw[:, :, :, s][:, None].to_broadcast([P, left, 2, CC]), ALU.mult).then_inc(S["fs_mul"], 1)
                    fill()
                    dve.wait_ge(S["fs_mul"], 3 * n + s + 1)
                    dst = uw[:, :, :, s + 1:C].rearrange("p x c j -> p j x c")
                    tt(dst, tmp, dst, ALU.add).then_inc(S["fs_add"], 1)
                    fill()

            def body(n, first, head, tail, second, store, more):
                c, d, z = n - 1, n - 2, n - ZL
                ALL = 5 * NC
                if early(n):
                    had_head, had_tail = parts(n - 1)[1:3]

                    first_left = EP[n - 1]["own"] if n > 0 else ALL

                    def one(i):
                        if first_left + i < ALL:
                            recurrence(c - 1, first_left + i, first_left + i + 1, had_head, had_tail)
                        else:
                            recurrence(c, first_left + i - ALL, first_left + i - ALL + 1, head, tail)

                    extra = ALL - first_left
                    position[0], end[0], before[0], issue[0] = 0, extra + EP[n]["own"], extra, one
                    statistics("A", n + 1)
                    normalised("A", n + 1)
                    first_sum(n)
                    upto(EL[n]["statistics_b"] - first_left)
                    statistics("B", n)
                    upto(EL[n]["norm_b"] - first_left)
                    normalised("B", n)
                    upto(EL[n]["routing_1"] - first_left)
                    routing(1, n + 1, xn1, m1_1)
                    upto(EL[n]["key_query"] - first_left)
                    key_and_query(n)
                    upto(extra + EP[n]["key_floor"])
                    key_floor(n)
                    upto(extra + EP[n]["key_inverse"])
                    key_inverse(n)
                    upto(extra + EP[n]["normal_key"])
                    normal_key(n)
                    fill()
                    key_gamma(n)
                    upto(extra + EP[n]["key_products"])
                    key_products(n)
                    upto(extra + EP[n]["solve"])
                    substitution(n)
                    upto(extra + EP[n]["own"])
                    if tail:
                        mix(d, 0)
                        mix(d, 1)
                        for s in range(C):
                            mixed(d, s)
                            if s < 2:
                                mix(d, s + 2)
                        statistics("C", d)
                    return
                dp, dq, extra = DP, DQ, 0
                if isinstance(n, int) and n == ZL:
                    dp, dq, extra = ZP, ZQ, ALL - EP[n - 1]["own"]
                    first_sum(n)
                if isinstance(n, int) and n >= NB:
                    dp, dq = LP, LQ

                def one(i):
                    if i < extra:
                        recurrence(c - 1, ALL - extra + i, ALL - extra + i + 1, True, True)
                    else:
                        recurrence(c, i - extra, i - extra + 1, head, tail)

                position[0], end[0], before[0], issue[0] = 0, ALL + extra, extra, one

                upto(dp["norm_c"])
                if second:
                    normalised("C", z)
                upto(dp["y2"])
                if second:
                    dve.wait_ge(S["wo_ps"], z + 1)
                    dve.wait_ge(S["y1_kept"], z + 1)
                    tt(y2T[:, :], p_wo, y1T[:, z, :], ALU.add).then_inc(S["y2"], 1)
                upto(dp["statistics_d"])
                if second:
                    statistics("D", z)
                upto(dp["norm_d"])
                if second:
                    normalised("D", z)
                if more:
                    statistics("A", n + 1)
                upto(dp["routing_2"])
                if second:
                    routing(2, z, xn2, m1_2)
                if more:
                    normalised("A", n + 1)
                upto(dp["y1"])
                if first and not (isinstance(n, int) and n == ZL):
                    first_sum(n)
                upto(dp["statistics_b"])

                if first:
                    statistics("B", n)
                upto(dq["norm_b"])
                if first:
                    normalised("B", n)
                upto(dq["routing_1"])
                if more:
                    routing(1, n + 1, xn1, m1_1)
                upto(dq["key_query"])
                if first:
                    key_and_query(n)
                upto(dq["key_floor"])
                if first:
                    key_floor(n)
                upto(dq["key_inverse"])
                if first:
                    key_inverse(n)
                upto(dq["mix"])
                if tail:
                    mix(d, 0)
                    fill()
                    mix(d, 1)
                    fill()
                    mixed(d, 0)
                    fill()
                if first:
                    normal_key(n)
                    fill()
                if tail:
                    mixed(d, 1)
                    fill()
                if first:
                    key_gamma(n)
                    fill()
                if tail:
                    mix(d, 2)
                    fill()
                    mix(d, 3)
                    fill()
                    mixed(d, 2)
                upto(dq["mixed"])
                if tail:
                    mixed(d, 3)
                upto(dq["key_products"])
                if first:
                    key_products(n)
                    fill()
                upto(dq["solve"])
                if second:
                    dve.wait_ge(S["down2"], NM * (z + 1))
                    if some(z):
                        dve.wait_ge(S["out_ps"], z)
                    stt(y3T[:, :], p_acc, hb2[:, :], y2T[:, :], ALU.add, ALU.add).then_inc(S["y3"], 1)
                if tail:
                    statistics("C", d)
                if first:
                    substitution(n)
                upto(ALL + extra)
            run(dve, body)

        @block.gpsimd
        def _(pool):
            tt = nc.gpsimd.tensor_tensor
            nc.gpsimd.memset(ident[:, :], 0.0).then_inc(S["consts_pool"], 1)
            nc.gpsimd.memset(average[:, :], 1.0 / D).then_inc(S["consts_pool"], 1)
            nc.gpsimd.memset(heads[:, :], 1.0).then_inc(S["consts_pool"], 1)
            pool.wait_ge(S["consts_pool"], 3)
            nc.gpsimd.affine_select(out=ident[:, :], in_=ident[:, :], compare_op=ALU.not_equal, fill=1.0, base=0,
                                    pattern=[[-1, P]], channel_multiplier=1).then_inc(S["setup_p"], 1)
            hv = heads[:, :].rearrange("p (h k) -> p h k", k=HD)
            nc.gpsimd.affine_select(out=hv, in_=hv, compare_op=ALU.is_ge, fill=0.0, base=0,
                                    pattern=[[-HD, H], [0, HD]], channel_multiplier=1).then_inc(S["consts_fold"], 1)
            pool.wait_ge(S["consts_fold"], 1)
            nc.gpsimd.affine_select(out=hv, in_=hv, compare_op=ALU.is_ge, fill=0.0, base=HD - 1,
                                    pattern=[[HD, H], [0, HD]], channel_multiplier=-1).then_inc(S["setup_p"], 1)

            def rest(tag, b, whole, one, dst):
                pool.wait_ge(S[f"m1_{tag}"], b + 1)
                tt(dst[:, :], whole[:, :], one[:, :], ALU.subtract).then_inc(S[f"m0_{tag}"], 1)

            rest(1, 0, xn1, m1_1, m0_1)

            def state_products(b, lo, hi, there):
                for i in range(lo, hi) if there else ():
                    if i == 0:
                        pool.wait_ge(S["carried"], b + 1)
                        if some(2 * b - 1):
                            pool.wait_ge(S["o_lane"], 2 * b - 1)
                    else:
                        pool.wait_ge(S["c_state"], NC * b + i)
                    if i == NC // 2 and some(2 * b):
                        pool.wait_ge(S["o_lane"], 2 * b)
                    if i in (0, SPLIT):
                        pool.wait_ge(S[("q_head", "q_tail")[i > 0]], 32 * (b + 1))
                    rows = slice(C * i, C * i + C)
                    tt(oprod[:, rows, :, :],
                       l_q[:, :, rows].rearrange("p k t -> p t k")[:, :, None, :].to_broadcast([P, C, HD // 2, HD]),
                       state[:, i].rearrange("p k v -> p v k")[:, None].to_broadcast([P, C, HD // 2, HD]),
                       ALU.mult).then_inc(S["oprod"], 1)
                    if i == NC // 2 - 1:
                        state_output(b, 0)
                    if i == NC - 1:
                        state_output(b, 1)

            def state_output(b, half):
                rows = slice(TB // 2 * half, TB // 2 * (half + 1))
                pool.wait_ge(S["oprod"], NC * b + NC // 2 * (half + 1))
                tt(osum4[:, :, :, :], oprod[:, rows, :, 0:4], oprod[:, rows, :, 4:8], ALU.add).then_inc(S["o_sum"], 1)
                pool.wait_ge(S["o_sum"], 4 * b + 2 * half + 1)
                tt(osum2[:, :, :, :], osum4[:, :, :, 0:2], osum4[:, :, :, 2:4], ALU.add).then_inc(S["o_sum"], 1)
                pool.wait_ge(S["o_sum"], 4 * b + 2 * half + 2)
                if some(16 * 8 * b):
                    pool.wait_ge(S["uo_back"], 16 * 8 * b)
                tt(uo_l[:, :, 1, rows].rearrange("p v t -> p t v"), osum2[:, :, :, 0], osum2[:, :, :, 1], ALU.add)\
                    .then_inc(S["o_lane"], 1)

            def decays(n):
                pool.wait_ge(S["f_sb"], n + 1)
                pool.wait_ge(S["fc0"], n + 1)
                for j in range(1, C):
                    if some(3 * n + j - 1):
                        pool.wait_ge(S["fc"], 3 * n + j - 1)
                    tt(steps(feat[:, FC, :])[:, j], steps(feat[:, FC, :])[:, j - 1], steps(f[:, :])[:, j], ALU.mult)\
                        .then_inc(S["fc"], 1)
                pool.wait_ge(S["q_sb"], n + 1)
                pool.wait_ge(S["fc"], 3 * (n + 1))
                tt(feat[:, QT, :], q[:, :], feat[:, FC, :], ALU.mult).then_inc(S["qt"], 1)
                pool.wait_ge(S["kn"], n + 1)
                for j in range(1, C):
                    if some(3 * n + j - 1):
                        pool.wait_ge(S["rr"], 3 * n + j - 1)
                    tt(keys[:, j, :, 0:j], keys[:, j - 1, :, 0:j],
                       steps(f[:, :])[:, j][:, :, None].to_broadcast([P, CC, j]), ALU.mult).then_inc(S["rr"], 1)
                pool.wait_ge(S["ag"], n + 1)
                if some(3 * n):
                    pool.wait_ge(S["ap"], 3 * n)
                tt(a[:, :], ag[:, :], f[:, :], ALU.mult).then_inc(S["a_sb"], 1)
                pool.wait_ge(S["a_sb"], n + 1)
                tt(feat[:, WW, :], a[:, :], feat[:, FC, :], ALU.mult).then_inc(S["wt"], 1)

            def query_products(n):
                pool.wait_ge(S["rr"], 3 * (n + 1))
                for s in range(C):
                    tt(qp[:, n, QPAIRS[s]:QPAIRS[s] + C - s, :], steps(q[:, :])[:, s:C], keys[:, s:C, :, s],
                       ALU.mult).then_inc(S["qp"], 1)

            def gated(d):
                pool.wait_ge(S["mix_add"], C * (d + 1))
                if some(d):
                    pool.wait_ge(S["tokC"], d)
                tt(o_g[:, :], uo_f[:, 1, :], og[:, d, :], ALU.mult).then_inc(S["o_g"], 1)

            def body(n, first, head, tail, second, store, more):
                c, d, z = n - 1, n - 2, n - ZL
                if early(n):
                    rest(1, n + 1, xn1, m1_1, m0_1)
                    state_products(d, early_chunks(n - 1), NC, tail)
                    decays(n)
                    query_products(n)
                    state_products(c, 0, early_chunks(n), head)
                    if tail:
                        gated(d)
                    return
                if isinstance(n, int) and n == ZL:
                    state_products(d, early_chunks(n - 1), SPLIT, True)
                state_products(d, SPLIT, NC, tail)
                state_products(c, 0, PP[0], head)
                if second:
                    rest(2, z, xn2, m1_2, m0_2)
                state_products(c, PP[0], PP[1], head)
                if more:
                    rest(1, n + 1, xn1, m1_1, m0_1)
                if first:
                    decays(n)
                if tail:
                    gated(d)
                if first:
                    query_products(n)
                state_products(c, PP[1], SPLIT, head)
            run(pool, body)


_INS = ["L0_attn_x", "L0_attn_Wq", "L0_attn_Wk", "L0_attn_Wv", "L0_attn_Wgamma", "L0_attn_Wf1", "L0_attn_Wf2",
        "L0_attn_Wog1", "L0_attn_Wog2", "L0_attn_norm_w", "L0_attn_Wo", "L0_ffn_gate_w", "L0_ffn_w1", "L0_ffn_b1",
        "L0_ffn_w2", "L0_ffn_b2", "L0_ffn_sw1", "L0_ffn_sb1", "L0_ffn_sw2", "L0_ffn_sb2"]


def kernel(**inputs):
    import numpy as _np
    import concourse.bacc as _bacc
    from concourse import mybir as _mybir
    from concourse.bass_utils import run_bass_kernel_spmd as _run

    nc = _bacc.Bacc("TRN2", target_bir_lowering=False, num_devices=1)
    arrays, args = {}, []
    for name in _INS:
        a = _np.ascontiguousarray(inputs[name])
        arrays[f"in_{name}"] = a
        args.append(nc.dram_tensor(f"in_{name}", a.shape, _mybir.dt.from_np(a.dtype), kind="ExternalInput").ap())
    args.append(nc.dram_tensor("out_dram", (B, T, D), F32, kind="ExternalOutput").ap())
    macaron_kernel(nc, *args)
    r = _run(nc, [arrays], core_ids=[0])
    return r.results[0]["out_dram"]
```
